# Optimizing a Trainium2 kernel written in Bass

```python
import numpy as np
import jax
import jax.numpy as jnp

def _softmax(x, axis=-1):
    return jax.nn.softmax(x, axis=axis)

def _gelu(x):
    return jax.nn.gelu(x, approximate=True)

def _silu(x):
    return jax.nn.silu(x)

def _sigmoid(x):
    return jax.nn.sigmoid(x)

def _layernorm(x, axis=-1, eps=1e-05):
    m = jnp.mean(x, axis=axis, keepdims=True)
    v = jnp.var(x, axis=axis, keepdims=True)
    return (x - m) / jnp.sqrt(v + eps)

def _scatter_add(tgt, idx, src, axis=0):
    return tgt.at[idx].add(src)

def _segment_sum(src, seg, n):
    return jax.ops.segment_sum(src, seg, n)
kernel_name = 'mk_adj_resnorm_d2_adj_r2_edbdba'

def setup_inputs(seed: int=0):
    np.random.seed(seed)
    _w = jnp.asarray

    def _rec_inputs():
        import jax
        import jax.numpy as jnp
        _gk = jax.random.key(seed)
        x = -0.0005207 + 1.001 * jax.random.normal(jax.random.fold_in(_gk, 1), (8192, 128), jnp.float32)
        _a = jax.random.bernoulli(jax.random.fold_in(_gk, 2), 0.000488281, (8192, 8192))
        _a = jnp.logical_or(_a, jnp.swapaxes(_a, -1, -2))
        _a = jnp.logical_or(_a, jnp.eye(8192, dtype=bool))
        adj = _a.astype(jnp.int32)
        return (x, adj)
    x, adj = _rec_inputs()

    def _L0_gnn_setup():
        import jax, jax.numpy as jnp
        import numpy as np
        ALPHA = 0.2
        MASK_VAL = -9000000000000000.0
        key = jax.random.key(seed)
        k1, k2, k3, k4 = jax.random.split(key, 4)
        N, Fin, Fout = (4096, 128, 128)
        h = jax.random.normal(k1, (N, Fin), dtype=jnp.float32)
        adj = jax.random.randint(k2, (N, N), 0, 2, dtype=jnp.int32)
        W = jax.random.normal(k3, (Fin, Fout), dtype=jnp.float32) * 0.06
        a = jax.random.normal(k4, (2 * Fout, 1), dtype=jnp.float32) * 0.06
        return {'h': h, 'adj': adj, 'W': W, 'a': a}
    _L0_gnn_all = _L0_gnn_setup()
    _L0_gnn_in = {k: v for k, v in _L0_gnn_all.items() if k in ('W', 'a')}
    del _L0_gnn_all

    def _L1_gnn_setup():
        import jax, jax.numpy as jnp
        import numpy as np
        N = 8192
        F_IN = 128
        F_OUT = 128
        key = jax.random.key(seed)
        k1, k2, k3 = jax.random.split(key, 3)
        x = jax.random.normal(k1, (N, F_IN), dtype=jnp.float32)
        adj = jax.random.randint(k2, (N, N), 0, 2, dtype=jnp.int32)
        stdv = np.sqrt(6.0 / (2 * F_IN + F_OUT)).astype(np.float32)
        weight = jax.random.uniform(k3, (2 * F_IN, F_OUT), dtype=jnp.float32, minval=-stdv, maxval=stdv)
        bias = jnp.zeros((F_OUT,), dtype=jnp.float32)
        return {'x': x, 'adj': adj, 'weight': weight, 'bias': bias}
    _L1_gnn_all = _L1_gnn_setup()
    _L1_gnn_in = {k: v for k, v in _L1_gnn_all.items() if k in ('weight', 'bias')}
    del _L1_gnn_all
    return {'x': x, 'adj': adj, 'L0_gnn_W': _L0_gnn_in['W'], 'L0_gnn_a': _L0_gnn_in['a'], 'L1_gnn_weight': _L1_gnn_in['weight'], 'L1_gnn_bias': _L1_gnn_in['bias']}

def reference(x, adj, L0_gnn_W, L0_gnn_a, L1_gnn_weight, L1_gnn_bias):
    import jax
    import jax.numpy as jnp

    def _L0_gnn_ref(h, adj, W, a):
        import jax, jax.numpy as jnp
        import numpy as np
        ALPHA = 0.2
        MASK_VAL = -9000000000000000.0
        Fout = W.shape[1]
        Wh = h @ W
        a1, a2 = (a[:Fout, 0], a[Fout:, 0])
        e = (Wh @ a1)[:, None] + (Wh @ a2)[None, :]
        e = jnp.where(e > 0, e, ALPHA * e)
        e = jnp.where(adj > 0, e, MASK_VAL)
        attention = jax.nn.softmax(e, axis=1)
        h_prime = attention @ Wh
        return jax.nn.elu(h_prime)

    def _L1_gnn_ref(x, adj, weight, bias):
        import jax, jax.numpy as jnp
        import numpy as np
        N = 8192
        F_IN = 128
        F_OUT = 128
        a = adj.astype(x.dtype)
        deg = jnp.sum(a, axis=1, keepdims=True)
        x1 = a @ x / deg
        n_x = jnp.concatenate([x1, x], axis=1)
        return n_x @ weight + bias
    x = _layernorm(x + _L0_gnn_ref(x, adj, L0_gnn_W, L0_gnn_a), axis=-1)
    x = _layernorm(x + _L1_gnn_ref(x, adj, L1_gnn_weight, L1_gnn_bias), axis=-1)
    return x

_drawn_inputs = setup_inputs


def setup_inputs(seed=0):
    import zlib

    import numpy as np

    out = dict(_drawn_inputs(seed))
    spreads = {'L1_gnn_bias': (0.0, 0.1)}
    factors = {}
    for name, (base, spread) in spreads.items():
        noise = np.random.default_rng([zlib.crc32(name.encode()), seed]).standard_normal(out[name].shape)
        drawn = base * np.exp(spread * noise) if base else spread * noise
        out[name] = jnp.asarray(drawn.astype(out[name].dtype))
    for name, factor in factors.items():
        out[name] = (out[name] * factor).astype(out[name].dtype)
    return out
```

```python
from contextlib import ExitStack

import concourse.bass as bass
from concourse import mybir

ALU = mybir.AluOpType
ACT = mybir.ActivationFunctionType
AX = mybir.AxisListType
F32 = mybir.dt.float32
BF16 = mybir.dt.bfloat16
F16 = mybir.dt.float16
F8 = mybir.dt.float8e4
U16 = mybir.dt.uint16
I32 = mybir.dt.int32

P = 128
BITS = 16
WPT = P // BITS
TPG = 2
GROUP = TPG * P
WPG = TPG * WPT
UNIT = 16
HALF = 8
MASK_SLOTS = 4
BIG = 2.0 ** 80
X_SCALE = 2.0 ** 11
E_SCALE = 2.0 ** 14
F8_ONE = 2.0 ** -9
ADJ_SLOTS = 2
RING_1 = 4
EPS = 1e-5
ALPHA = 0.2


def adj_resnorm_kernel(nc, x, adj, w0, a0, w1, b1, consts, out):
    N, F = x.shape
    NG = N // GROUP
    NJ = N // P
    UPG = NJ // UNIT
    FD = F + 1
    ROW = 2 * FD
    XB = 4
    NX = NJ // XB
    X_SLOTS = 4
    COLS = UNIT * P
    WPU = UNIT * WPG

    s_dram = nc.dram_tensor("s_rows", [NJ, P], F32, kind="Internal").ap()
    x1_dram = nc.dram_tensor("x1_rows", [N, F], F32, kind="Internal").ap()
    parts_dram = nc.dram_tensor("x1_parts", [N, ROW], F16, kind="Internal").ap()

    ctx = ExitStack()
    with ctx:
        def sb(name, shape, dt):
            return ctx.enter_context(nc.sbuf_tensor(name, shape, dt))

        def sem(name):
            return ctx.enter_context(nc.semaphore(name))

        words = sb("words", [P, NG, NJ * WPG], U16)
        factors = sb("factors", [P, 2, NJ, ROW], F16)
        adj_ring = sb("adj_ring", [P, ADJ_SLOTS, TPG, COLS], I32)
        neg_ring = sb("neg_ring", [P, 2, UNIT, GROUP], BF16)
        pos_ring = sb("pos_ring", [P, MASK_SLOTS, HALF, GROUP], BF16)
        consts_sb = sb("consts_sb", [P, P + WPT], F32)
        pack_w = sb("pack_w", [P, WPT], BF16)
        s_row = sb("s_row", [P, 2, GROUP], F32)
        cols = sb("cols", [P, 12, NJ], F32)
        one = sb("one", [P, 24], F32)
        mean_row = sb("mean_row", [P, FD], F32)
        bias_row = sb("bias_row", [P, F], F32)
        w1_sb = sb("w1_sb", [P, 2, F], F32)
        part_sums = sb("part_sums", [P, TPG, ROW], F32)
        row_sums = sb("row_sums", [P, TPG, ROW], F32)
        rows_x = sb("rows_x", [P, TPG, F], F32)
        rows_y = sb("rows_y", [P, TPG, F], F32)
        parts = sb("parts", [P, TPG, ROW], F16)
        stats = sb("stats", [P, TPG, 6], F32)
        mv = sb("mv", [P, TPG, 2], F32)
        wh_top = sb("wh_top", [P, NX], F32)
        x_sums = sb("x_sums", [P, NX], F32)

        ident = consts_sb[:, 0:P]
        s_col, t_col, t_big, e_col, f_col, u_col, v_col, y_col, uy_col, vy_col, e_den, f_den = \
            (cols[:, k, :] for k in range(12))
        t_max, t_top, wh_max, wh_one, neg_t, neg_ft, inv_wh, scale_e, ones, sum_x = (one[:, k:k + 1] for k in range(10))
        minus_half, inv_den, flag, var_eps, rstd, minus_mean, shift = (one[:, k:k + 2] for k in range(10, 24, 2))
        nd = row_sums[:, :, 0:FD]
        hidden = row_sums[:, :, 0:F]
        exp_in = part_sums[:, :, 0:F]

        wh = words[:, NG // 2:, :].rearrange("p g w -> p (g w)").bitcast(F32)[:, 0:NJ * F]\
            .rearrange("p (j f) -> p j f", f=F)
        early = words[:, 2:NG // 2, :].rearrange("p g w -> p (g w)").bitcast(F32)
        sizes, at, early_of = dict(product=2 * UNIT * F, x_t=2 * XB * F, wq=F + 2, w_turn=P, a_sb=2,
                                   s_turn=P, sum_xb=P), 0, {}
        for name, size in sizes.items():
            early_of[name] = early[:, at:at + size]
            at += size
        product = early_of["product"].rearrange("p (k j f) -> p k j f", k=2, f=F)
        x_in = factors[:, 1, :, :].rearrange("p j r -> p (j r)").bitcast(F32)[:, 0:X_SLOTS * XB * F]\
            .rearrange("p (k j f) -> p k j f", k=X_SLOTS, f=F)
        x_t = early_of["x_t"].rearrange("p (k n) -> p k n", k=2)
        wq, w_turn, a_sb, s_turn, sum_xb = (early_of[n] for n in ("wq", "w_turn", "a_sb", "s_turn", "sum_xb"))
        ring_1 = adj_ring[:, :, :, :].rearrange("p s t c -> p (s t c)").bitcast(BF16)\
            .rearrange("p (s j r) -> p s j r", s=RING_1, j=UNIT)
        turned = pos_ring[:, 0, :, :].rearrange("p j r -> p (j r)").bitcast(F32)[:, 0:2 * TPG * P]

        acc = [ctx.enter_context(nc.psum_tensor(f"acc{k}", [P, 512], F32)) for k in range(2 * TPG)]
        pack_ps = [ctx.enter_context(nc.psum_tensor(f"pack_ps{k}", [P, 512], F32)) for k in range(2)]
        turn_ps = [ctx.enter_context(nc.psum_tensor(f"turn_ps{k}", [P, 512], F32)) for k in range(2)]

        consts_in, w0_in, a0_in, w1_in, bias_in = (sem(n) for n in "consts_in w0_in a0_in w1_in bias_in".split())
        x_in_sem = [sem(f"x_in{k}") for k in range(X_SLOTS)]
        adj_in = [sem("adj_in0"), sem("adj_in1")]
        s_row_in = [sem("s_row_in0"), sem("s_row_in1")]
        rows_in, rows1_in = sem("rows_in"), sem("rows1_in")
        parts_in = [sem(f"parts_in{k}") for k in range(NJ // HALF)]
        s_out, x1_out, parts_out, y_out = (sem(n) for n in "s_out x1_out parts_out y_out".split())
        pack_w_ok, ones_ok, half_ok, tail_ok = (sem(n) for n in "pack_w_ok ones_ok half_ok tail_ok".split())
        w_turned, w_turn_ok, wa_made, wa_ok = (sem(n) for n in "w_turned w_turn_ok wa_made wa_ok".split())
        x_turned, x_t_ok, wh_made, wh_ok, top_ok = (sem(n) for n in "x_turned x_t_ok wh_made wh_ok top_ok".split())
        s_turned, s_turn_ok, sum_x_ok, sum_xb_ok = (sem(n) for n in "s_turned s_turn_ok sum_x_ok sum_xb_ok".split())
        mean_made, mean_ok, one_row_ok = (sem(n) for n in "mean_made mean_ok one_row_ok".split())
        t_top_ok, t_max_ok, wh_one_ok, wh_max_ok = (sem(n) for n in "t_top_ok t_max_ok wh_one_ok wh_max_ok".split())
        neg_ok, y_ok_col, uy_ok, exp_cols_ok, t_big_ok = (sem(n) for n in "neg_ok y_col_ok uy_ok exp_cols_ok t_big_ok".split())
        guard_ok, inv_ok, scale_ok, den_ok, den_hi_ok = (sem(n) for n in "guard_ok inv_ok scale_ok den_ok den_hi_ok".split())
        ef_ok, product_ok, high_ok, factors_ok = (sem(n) for n in "ef_ok product_ok high_ok factors_ok".split())
        packed, words_ok, unpacked = (sem(n) for n in "packed words_ok unpacked".split())
        score_ok, pos_ok, mask_ok, mask_used, acc_done = (sem(n) for n in "score_ok pos_ok mask_ok mask_used acc_done".split())
        pos_copied, neg_added, nd_ok, flag_ok, full_ok, inv_den_ok, hidden_ok, exp_in_ok, exp_ok, elu_ok = (
            sem(n) for n in "pos_copied neg_added nd_ok flag_ok full_ok inv_den_ok hidden_ok exp_in_ok exp_ok elu_ok".split())
        y_ok, stats_ok, mv_ok, var_ok, rstd_ok, minus_ok, shift_ok, x1_ok, high_part, low_part = (
            sem(n) for n in "y_ok stats_ok mv_ok var_ok rstd_ok minus_ok shift_ok x1_ok high_part low_part".split())
        mask1_ok, mask1_used, acc1_done, copied1, nd1_ok, inv1_ok, mean1_ok, turned1, turned1_ok, proj1_ok, xb1_ok = (
            sem(n) for n in ("mask1_ok mask1_used acc1_done copied1 nd1_ok inv1_ok mean1_ok turned1 turned1_ok "
                             "proj1_ok xb1_ok").split())
        y1_ok, stats1_ok, mv1_ok, var1_ok, rstd1_ok, out_ok = (
            sem(n) for n in "y1_ok stats1_ok mv1_ok var1_ok rstd1_ok out_ok".split())

        x_tiles = x.rearrange("(j p) f -> p j f", p=P)
        adj_tiles = adj.rearrange("(g k t w) c -> g t k w c", g=NG, k=BITS, t=TPG)
        out_rows = out.rearrange("(g b p) f -> g p b f", g=NG, p=P)
        x_rows = x.rearrange("(g b p) f -> g p b f", g=NG, p=P)
        x1_rows = x1_dram.rearrange("(g b p) f -> g p b f", g=NG, p=P)
        parts_rows = parts_dram.rearrange("(g b p) f -> g p b f", g=NG, p=P)
        parts_tiles = parts_dram.rearrange("(j p) f -> p j f", p=P)
        s_rows = s_dram.rearrange("(g j) p -> g (j p)", g=NG)

        block = ctx.enter_context(nc.Block())

        @block.sync
        def _(sp):
            def load_adj(g, c):
                sp.wait_ge(packed, UPG * g + c + 1)
                for t in range(TPG):
                    sp.dma_start(adj_ring[:, c % ADJ_SLOTS, t, :],
                                 adj_tiles[g, t, :, :, c * COLS:(c + 1) * COLS])\
                        .then_inc(adj_in[c % ADJ_SLOTS], 16)

            def load_s(g, slot):
                sp.dma_start(s_row[:, slot, :], s_rows[g, :].partition_broadcast(P)).then_inc(s_row_in[slot], 16)

            def store_x1(g):
                sp.wait_ge(x1_ok, TPG * (g + 1))
                sp.dma_start(x1_rows[g], rows_y[:, :, :]).then_inc(x1_out, 16)
                sp.wait_ge(low_part, g + 1)
                sp.dma_start(parts_rows[g], parts[:, :, :]).then_inc(parts_out, 16)

            def load_x(g, first=False):
                if not first:
                    sp.wait_ge(y_ok, g)
                sp.dma_start(rows_x[:, :, :], x_rows[g]).then_inc(rows_in, 16)

            sp.sem_inc(packed, ADJ_SLOTS)
            sp.dma_start(consts_sb[:, :], consts).then_inc(consts_in, 16)
            sp.dma_start(wq[:, 0:F], w0).then_inc(w0_in, 16)
            sp.dma_start(a_sb, a0.rearrange("(k f) o -> f (k o)", k=2), allow_slow_non_contiguous=True).then_inc(a0_in, 16)
            for k in range(X_SLOTS):
                sp.dma_start(x_in[:, k], x_tiles[:, XB * k:XB * (k + 1), :]).then_inc(x_in_sem[k], 16)
            load_adj(0, 0)
            load_adj(0, 1)
            with sp.Fori(1, NX // X_SLOTS) as n:
                for k in range(X_SLOTS):
                    sp.wait_ge(x_turned, X_SLOTS * (n - 1) + k + 1)
                    sp.dma_start(x_in[:, k], x_tiles[:, bass.ds(XB * (X_SLOTS * n + k), XB), :])\
                        .then_inc(x_in_sem[k], 16)
            sp.dma_start(w1_sb[:, :, :], w1.rearrange("(k f) o -> f k o", k=2)).then_inc(w1_in, 16)
            sp.dma_start(bias_row[:, :], b1.partition_broadcast(P)).then_inc(bias_in, 16)
            sp.wait_ge(s_turn_ok, 1)
            sp.dma_start(s_dram, s_turn[0:NJ, :]).then_inc(s_out, 16)
            sp.wait_ge(s_out, 16)
            load_s(0, 0)
            load_s(1, 1)
            load_x(0, True)
            load_adj(0, 2)
            load_adj(0, 3)

            def group(g, slot, first=False, adj_next=True, s_next=True):
                if adj_next:
                    for c in range(UPG):
                        load_adj(g + 1, c)
                if not first:
                    store_x1(g - 1)
                    load_x(g)
                if s_next:
                    sp.wait_ge(score_ok, 8 * (g + 1))
                    load_s(g + 2, slot)

            group(0, 0, first=True)
            with sp.Fori(0, NG // 2 - 2) as n:
                group(2 * n + 1, 1)
                group(2 * n + 2, 0)
            group(NG - 3, 1)
            group(NG - 2, 0, s_next=False)
            group(NG - 1, 1, adj_next=False, s_next=False)

            sp.wait_ge(mask_used, 8 * NG + MASK_SLOTS)
            sp.wait_ge(parts_out, 16 * (NG - 1))
            for k in range(NJ // HALF):
                if k == NJ // HALF - 1:
                    store_x1(NG - 1)
                    sp.wait_ge(parts_out, 16 * NG)
                sp.dma_start(factors[:, 0, HALF * k:HALF * (k + 1), :], parts_tiles[:, HALF * k:HALF * (k + 1), :])\
                    .then_inc(parts_in[k], 16)
            sp.wait_ge(x1_out, 16 * NG)

            def rows_1(g):
                sp.dma_start(rows_x[:, :, :], x1_rows[g]).then_inc(rows1_in, 16)

            def store_1(g):
                sp.wait_ge(out_ok, TPG * (g + 1))
                sp.dma_start(out_rows[g], rows_y[:, :, :]).then_inc(y_out, 16)

            rows_1(0)
            with sp.Fori(1, NG) as g:
                sp.wait_ge(turned1, g)
                sp.wait_ge(xb1_ok, g)
                rows_1(g)
                store_1(g - 1)
            store_1(NG - 1)
            sp.wait_ge(y_out, 16 * NG)

        @block.gpsimd
        def _(pool):
            pool.memset(minus_half, -0.5).then_inc(half_ok, 1)
            pool.wait_ge(t_top_ok, 1)
            pool.partition_all_reduce(t_max, t_top, P, bass.bass_isa.ReduceOp.max).then_inc(t_max_ok, 1)
            pool.wait_ge(wh_one_ok, 1)
            pool.partition_all_reduce(wh_max, wh_one, P, bass.bass_isa.ReduceOp.max).then_inc(wh_max_ok, 1)

            def inverse_deviation(n, mv_sem, var_sem, rstd_sem):
                pool.wait_ge(half_ok, 1)
                pool.wait_ge(mv_sem, n)
                pool.tensor_scalar(var_eps, mv[:, :, 1], EPS, None, ALU.add).then_inc(var_sem, TPG)
                pool.wait_ge(var_sem, n)
                pool.tensor_tensor(rstd, var_eps, minus_half, ALU.pow).then_inc(rstd_sem, TPG)

            with pool.Fori(TPG, TPG * NG + 1, TPG) as n:
                inverse_deviation(n, mv_ok, var_ok, rstd_ok)
                pool.tensor_scalar(minus_mean, mv[:, :, 0], -1.0, None, ALU.mult).then_inc(minus_ok, TPG)
                pool.wait_ge(minus_ok, n)
                pool.wait_ge(rstd_ok, n)
                pool.tensor_tensor(shift, minus_mean, rstd, ALU.mult).then_inc(shift_ok, TPG)
            with pool.Fori(TPG, TPG * NG + 1, TPG) as n:
                inverse_deviation(n, mv1_ok, var1_ok, rstd1_ok)

        @block.scalar
        def _(act):
            act.wait_ge(consts_in, 16)
            act.activation(pack_w[:, :], consts_sb[:, P:P + WPT], ACT.Copy).then_inc(pack_w_ok, 1)
            act.wait_ge(w_turned, 1)
            act.activation(w_turn, turn_ps[0][:, 0:P], ACT.Copy).then_inc(w_turn_ok, 1)
            act.wait_ge(wa_made, 1)
            act.activation(wq[:, F:F + 2], turn_ps[1][:, 0:2], ACT.Copy).then_inc(wa_ok, 1)

            def copy_turned(n, first=False):
                for k in range(2):
                    act.wait_ge(x_turned, 2 * n + k + 1)
                    if not first:
                        act.wait_ge(wh_made, 2 * n + k - 1)
                    act.activation(x_t[:, k, :], turn_ps[k][:, :], ACT.Copy,
                                   accum_out=x_sums[:, bass.ds(2 * n + k, 1)]).then_inc(x_t_ok, 1)

            def copy_words(g, c):
                act.wait_ge(packed, UPG * g + c + 1 + ADJ_SLOTS)
                act.activation(words[:, g, c * WPU:(c + 1) * WPU], pack_ps[c % 2][:, 0:WPU], ACT.Copy)\
                    .then_inc(words_ok, 1)

            copy_turned(0, True)
            with act.Fori(1, NX // 2) as n:
                copy_turned(n)
            act.wait_ge(s_turned, 1)
            act.activation(s_turn[0:NJ, :], turn_ps[0][0:NJ, 0:P], ACT.Copy).then_inc(s_turn_ok, 1)
            copy_words(0, 0)
            copy_words(0, 1)

            act.wait_ge(neg_ok, 2)
            act.activation(e_col, t_col, ACT.Exp, bias=neg_t).then_inc(exp_cols_ok, 1)
            act.activation(f_col, t_col, ACT.Exp, bias=neg_ft, scale=ALPHA).then_inc(exp_cols_ok, 1)
            act.wait_ge(uy_ok, 2)
            act.activation(u_col, uy_col, ACT.Exp).then_inc(exp_cols_ok, 1)
            act.activation(v_col, vy_col, ACT.Exp).then_inc(exp_cols_ok, 1)
            act.wait_ge(t_big_ok, 1)

            def scores(g, slot, h):
                act.wait_ge(mask_used, 8 * g + h + 1)
                for j in range(HALF):
                    a = act.activation(pos_ring[:, h % MASK_SLOTS, j, :], s_row[:, slot, :], ACT.Relu,
                                       bias=t_big[:, h * HALF + j:h * HALF + j + 1], scale=BIG)
                a.then_inc(score_ok, 1)

            def copy_positive(g, first=False):
                if not first:
                    act.wait_ge(elu_ok, g)
                for b in range(TPG):
                    act.wait_ge(acc_done, 3 * g + 2 * b + 1)
                    act.activation(part_sums[:, b, :], acc[2 * b][:, 0:ROW], ACT.Copy,
                                   scale=u_col[:, bass.ds(TPG * g + b, 1)]).then_inc(pos_copied, 1)

            def exponential(g):
                act.wait_ge(exp_in_ok, g + 1)
                act.activation(exp_in, exp_in, ACT.Exp).then_inc(exp_ok, 1)

            def high_parts(g, first=False):
                act.wait_ge(x1_ok, TPG * (g + 1))
                if first:
                    act.wait_ge(tail_ok, 2)
                else:
                    act.wait_ge(parts_out, 16 * g)
                act.activation(parts[:, :, 0:F], rows_y[:, :, :], ACT.Copy, scale=X_SCALE).then_inc(high_part, 1)

            def next_words(g, c, last=False):
                if not (last and c >= 2):
                    copy_words(g + c // 2, (c + 2) % UPG)

            def normalise(g, first=False):
                act.wait_ge(shift_ok, TPG * (g + 1))
                if not first:
                    act.wait_ge(low_part, g)
                for b in range(TPG):
                    act.activation(rows_y[:, b, :], rows_y[:, b, :], ACT.Identity, bias=shift[:, b:b + 1],
                                   scale=rstd[:, b:b + 1]).then_inc(x1_ok, 1)

            def group(g, slot, loads, second=False, last=False):
                act.wait_ge(s_row_in[slot], 16 * loads)
                for h in range(8):
                    scores(g, slot, h)
                    if h % 2:
                        next_words(g, h // 2, last)
                    if h == 2:
                        copy_positive(g - 1, second)
                    if h == 4:
                        exponential(g - 1)
                    if h == 6:
                        normalise(g - 1, second)
                    if h == 7:
                        high_parts(g - 1, second)

            act.wait_ge(s_row_in[0], 16)
            for c in range(UPG):
                for k in range(2):
                    act.wait_ge(product_ok, 2 * c + k + 1)
                    act.activation(factors[:, k, c * UNIT:(c + 1) * UNIT, 0:F], product[:, k, :, :], ACT.Copy)\
                        .then_inc(high_ok, 1)
                for h in (2 * c, 2 * c + 1):
                    scores(0, 0, h)
                next_words(0, c)
            act.wait_ge(factors_ok, 2 * UPG)
            group(1, 1, 1, second=True)
            with act.Fori(1, NG // 2 - 1) as n:
                group(2 * n, 0, n + 1)
                group(2 * n + 1, 1, n + 1)
            group(NG - 2, 0, NG // 2)
            group(NG - 1, 1, NG // 2, last=True)
            copy_positive(NG - 1)
            exponential(NG - 1)
            normalise(NG - 1)
            high_parts(NG - 1)

            def copy_sums(g, first=False):
                if first:
                    act.wait_ge(elu_ok, NG)
                else:
                    act.wait_ge(nd1_ok, g)
                act.wait_ge(acc1_done, g + 1)
                act.activation(part_sums[:, 0, :], acc[0][:, 0:ROW], ACT.Copy).then_inc(copied1, 1)
                act.wait_ge(mask1_used, UPG * (g + 1) + RING_1)
                act.activation(part_sums[:, 1, :], acc[1][:, 0:ROW], ACT.Copy).then_inc(copied1, 1)

            def copy_turned_1(g, first=False):
                act.wait_ge(turned1, g + 1)
                if not first:
                    act.wait_ge(proj1_ok, g)
                act.activation(turned, turn_ps[0][:, :], ACT.Copy).then_inc(turned1_ok, 1)

            copy_sums(0, True)
            copy_turned_1(0, True)
            with act.Fori(1, NG) as g:
                copy_sums(g)
                copy_turned_1(g)

        @block.tensor
        def _(pe):
            pe.sem_inc(mask_used, MASK_SLOTS)
            pe.sem_inc(mask1_used, RING_1)
            pe.wait_ge(consts_in, 16)
            pe.wait_ge(w0_in, 16)
            pe.transpose(turn_ps[0][:, 0:P], wq[:, 0:F], ident).then_inc(w_turned, 1)
            pe.wait_ge(w_turn_ok, 1)
            pe.wait_ge(a0_in, 16)
            pe.matmul(turn_ps[1][:, 0:2], w_turn, a_sb, start=True, stop=True).then_inc(wa_made, 1)
            pe.wait_ge(wa_ok, 1)
            pe.wait_ge(ones_ok, 1)

            def turn_x(n, k, first=False):
                pe.wait_ge(x_in_sem[k], 16 * (n + 1))
                if not first:
                    pe.wait_ge(x_t_ok, X_SLOTS * n + k - 1)
                for j in range(XB):
                    m = pe.transpose(turn_ps[k % 2][:, j * P:(j + 1) * P], x_in[:, k, j, :], ident)
                m.then_inc(x_turned, 1)

            def make_wh(n, k, first=False):
                pe.wait_ge(x_t_ok, X_SLOTS * n + k + 1)
                if not first:
                    pe.wait_ge(wh_ok, X_SLOTS * n + k - 1)
                for j in range(XB):
                    o = (j % 2) * (F + 2)
                    m = pe.matmul(acc[2 * (k % 2) + j // 2][:, o:o + F + 2], x_t[:, k % 2, j * P:(j + 1) * P], wq,
                                  start=True, stop=True)
                m.then_inc(wh_made, 1)

            def wh_steps(n, first=False, last=False):
                for k in range(X_SLOTS):
                    if k + 1 < X_SLOTS:
                        turn_x(n, k + 1, first and k == 0)
                    elif not last:
                        turn_x(n + 1, 0)
                    make_wh(n, k, first and k < 2)

            turn_x(0, 0, True)
            wh_steps(0, first=True)
            with pe.Fori(1, NX // X_SLOTS - 1) as n:
                wh_steps(n)
            wh_steps(NX // X_SLOTS - 1, last=True)
            pe.wait_ge(wh_ok, NX)
            pe.transpose(turn_ps[0][0:NJ, 0:P], s_col, ident).then_inc(s_turned, 1)
            pe.wait_ge(pack_w_ok, 1)

            def packable(g, c, first=False):
                pe.wait_ge(adj_in[c % ADJ_SLOTS], 32 * (UPG // ADJ_SLOTS * g + c // ADJ_SLOTS + 1))
                if not first:
                    pe.wait_ge(words_ok, UPG * g + c - 1)

            def pack(c):
                for j in range(UNIT):
                    for t in range(TPG):
                        o = (j * TPG + t) * WPT
                        low_bytes = adj_ring[:, c % ADJ_SLOTS, t, j * P:(j + 1) * P].bitcast(F8)\
                            .rearrange("p (c b) -> p c b", b=4)[:, :, 0]
                        m = pe.matmul(pack_ps[c % 2][:, o:o + WPT], low_bytes, pack_w[:, :], start=True, stop=True)
                m.then_inc(packed, 1)

            for c in range(UPG):
                packable(0, c, first=(c < 2))
                pack(c)
            pe.wait_ge(sum_xb_ok, 1)
            pe.matmul(turn_ps[1][:, 0:F], sum_xb, wq[:, 0:F], start=True, stop=True).then_inc(mean_made, 1)

            def multiply(g, h, first=False):
                pe.wait_ge(mask_ok, 8 * g + h + 1)
                for a in range(2 * TPG):
                    b, neg = a // 2, a % 2
                    if h == 0 and not first:
                        pe.wait_ge(neg_added if neg else pos_copied, TPG * (g - 1) + b + 1)
                    for j in range(HALF):
                        jj = h * HALF + j
                        mask = neg_ring[:, (h // 2) % 2, (h % 2) * HALF + j, b * P:(b + 1) * P] if neg else \
                            pos_ring[:, h % MASK_SLOTS, j, b * P:(b + 1) * P]
                        m = pe.matmul(acc[a][:, 0:ROW], mask, factors[:, neg, jj, :],
                                      start=(jj == 0), stop=(jj == NJ - 1))
                    if h == 7 and a < 2 * TPG - 1:
                        m.then_inc(acc_done, 1)
                m.then_inc(mask_used, 1)

            def group(g, first=False, last=False):
                for c in range(UPG):
                    for h in (2 * c, 2 * c + 1):
                        if first and h % 2 == 0:
                            pe.wait_ge(factors_ok, 2 * (c + 1))
                        if h % 2 and not last:
                            packable(g + 1, c)
                        multiply(g, h, first)
                    if not last:
                        pack(c)

            pe.wait_ge(den_hi_ok, 4)
            group(0, first=True)
            with pe.Fori(1, NG - 1) as g:
                group(g)
            group(NG - 1, last=True)

            def multiply_1(g, c, first=False):
                pe.wait_ge(mask1_ok, UPG * g + c + 1)
                for b in range(TPG):
                    if c == 0 and first:
                        pe.wait_ge(neg_added if b else pos_copied, TPG * (NG - 1) + 1)
                    elif c == 0:
                        pe.wait_ge(copied1, TPG * (g - 1) + b + 1)
                    for j in range(UNIT):
                        jj = c * UNIT + j
                        if first and b == 0 and j % HALF == 0:
                            pe.wait_ge(parts_in[jj // HALF], 16)
                        m = pe.matmul(acc[b][:, 0:ROW], ring_1[:, c, j, b * P:(b + 1) * P], factors[:, 0, jj, :],
                                      start=(jj == 0), stop=(jj == NJ - 1))
                    if c == UPG - 1 and b == 0:
                        m.then_inc(acc1_done, 1)
                m.then_inc(mask1_used, 1)

            def turn_rows(g, first=False):
                pe.wait_ge(mean1_ok, TPG * (g + 1))
                pe.wait_ge(rows1_in, 16 * (g + 1))
                if not first:
                    pe.wait_ge(turned1_ok, g)
                for k, rows in enumerate((hidden, rows_x)):
                    for b in range(TPG):
                        m = pe.transpose(turn_ps[0][:, (TPG * k + b) * P:(TPG * k + b + 1) * P], rows[:, b, :], ident)
                m.then_inc(turned1, 1)

            def project(g, first=False):
                pe.wait_ge(turned1_ok, g + 1)
                if not first:
                    pe.wait_ge(y1_ok, g)
                for b in range(TPG):
                    for k in range(2):
                        m = pe.matmul(turn_ps[1][:, b * F:(b + 1) * F],
                                      turned[:, (TPG * k + b) * P:(TPG * k + b + 1) * P], w1_sb[:, k, :],
                                      start=(k == 0), stop=(k == 1))
                m.then_inc(proj1_ok, 1)

            def group_1(g, first=False, second=False):
                for c in range(UPG):
                    multiply_1(g, c, first)
                    if c == 0 and not first:
                        turn_rows(g - 1, second)
                    if c == 1 and not first:
                        project(g - 1, second)

            pe.wait_ge(w1_in, 16)
            group_1(0, first=True)
            group_1(1, second=True)
            with pe.Fori(2, NG) as g:
                group_1(g)
            turn_rows(NG - 1)
            project(NG - 1)

        @block.vector
        def _(dve):
            dve.memset(ones, 1.0).then_inc(ones_ok, 1)
            dve.memset(mean_row[:, F:FD], 1.0).then_inc(one_row_ok, 1)
            dve.memset(parts[:, :, F:FD], 1.0).then_inc(tail_ok, 1)
            dve.memset(parts[:, :, ROW - 1:ROW], 0.0).then_inc(tail_ok, 1)

            def copy_wh(n, k):
                dve.wait_ge(wh_made, 2 * n + k + 1)
                for half in range(2):
                    bank = acc[2 * k + half][:, 0:2 * (F + 2)].rearrange("p (j f) -> p j f", j=2)
                    j0 = 2 * XB * n + XB * k + 2 * half
                    dve.tensor_copy(wh[:, bass.ds(j0, 2), :], bank[:, :, 0:F])
                    d = dve.tensor_copy(cols[:, 0:2, bass.ds(j0, 2)], bank[:, :, F:F + 2].rearrange("p j k -> p k j"))
                d.then_inc(wh_ok, 1)
                dve.wait_ge(wh_ok, 2 * n + k + 1)
                dve.tensor_reduce(wh_top[:, bass.ds(2 * n + k, 1)], wh[:, bass.ds(2 * XB * n + XB * k, XB), :], AX.XY,
                                  ALU.max, apply_absolute_value=True).then_inc(top_ok, 1)

            with dve.Fori(0, NX // 2) as n:
                for k in range(2):
                    copy_wh(n, k)
            dve.tensor_reduce(t_top, t_col, AX.X, ALU.max).then_inc(t_top_ok, 1)
            dve.wait_ge(top_ok, NX)
            dve.tensor_reduce(wh_one, wh_top[:, :], AX.X, ALU.max).then_inc(wh_one_ok, 1)
            dve.tensor_scalar(t_big, t_col, BIG, None, ALU.mult).then_inc(t_big_ok, 1)
            dve.wait_ge(x_t_ok, NX)
            dve.tensor_reduce(sum_x, x_sums[:, :], AX.X, ALU.add).then_inc(sum_x_ok, 1)
            dve.wait_ge(sum_x_ok, 1)
            dve.tensor_scalar(sum_xb, ident, 0.0, sum_x, ALU.mult, ALU.add).then_inc(sum_xb_ok, 1)

            dve.wait_ge(t_max_ok, 1)
            dve.tensor_scalar(neg_t, t_max, -1.0, None, ALU.mult).then_inc(neg_ok, 1)
            dve.tensor_scalar(neg_ft, t_max, -ALPHA, None, ALU.mult).then_inc(neg_ok, 1)
            dve.tensor_scalar(y_col, s_col, t_max, None, ALU.add).then_inc(y_ok_col, 1)
            dve.wait_ge(y_ok_col, 1)
            dve.tensor_scalar(uy_col, y_col, 1.0 - ALPHA, 0.0, ALU.mult, ALU.min).then_inc(uy_ok, 1)
            dve.tensor_scalar(vy_col, y_col, ALPHA - 1.0, 0.0, ALU.mult, ALU.min).then_inc(uy_ok, 1)
            dve.wait_ge(wh_max_ok, 1)
            dve.tensor_scalar(wh_one, wh_max, 1e-30, None, ALU.max).then_inc(guard_ok, 1)
            dve.wait_ge(guard_ok, 1)
            dve.reciprocal(inv_wh, wh_one).then_inc(inv_ok, 1)
            dve.wait_ge(inv_ok, 1)
            dve.tensor_scalar(scale_e, inv_wh, E_SCALE, None, ALU.mult).then_inc(scale_ok, 1)
            dve.wait_ge(exp_cols_ok, 2)
            dve.wait_ge(scale_ok, 1)
            for k, (col, den) in enumerate(((e_col, e_den), (f_col, f_den))):
                dve.tensor_scalar(den, col, E_SCALE, None, ALU.mult).then_inc(den_ok, 1)
                dve.wait_ge(den_ok, k + 1)
                dve.tensor_copy(factors[:, k, :, F], den).then_inc(den_hi_ok, 1)
                dve.wait_ge(den_hi_ok, 2 * k + 1)
                dve.tensor_tensor(factors[:, k, :, ROW - 1], den, factors[:, k, :, F], ALU.subtract)\
                    .then_inc(den_hi_ok, 1)
                dve.tensor_scalar(col, col, scale_e, None, ALU.mult).then_inc(ef_ok, 1)

            dve.wait_ge(mean_made, 1)
            dve.tensor_scalar(mean_row[:, 0:F], turn_ps[1][:, 0:F], 1.0 / N, inv_wh, ALU.mult, ALU.mult)\
                .then_inc(mean_ok, 1)

            def unpack(g, c, ring, slot):
                src = words[:, g, c * WPU:(c + 1) * WPU].rearrange("p (j w) -> p j w", j=UNIT)
                dst = ring[:, slot, :, :].bitcast(U16)
                for k in range(BITS):
                    to = dst[:, :, k * WPG:(k + 1) * WPG]
                    if k < 14:
                        d = dve.tensor_scalar(to, src, 14 - k, 0x4000, ALU.logical_shift_left, ALU.bitwise_and)
                    else:
                        d = dve.tensor_scalar(to, src, k - 14, 0x4000, ALU.logical_shift_right, ALU.bitwise_and)
                return d

            def masks(g, c, words_count):
                dve.wait_ge(mask_used, 8 * g + 2 * c + 2)
                dve.wait_ge(words_ok, words_count)
                unpack(g, c, neg_ring, c % 2).then_inc(unpacked, 1)
                dve.wait_ge(unpacked, UPG * g + c + 1)
                halves = [(8 * g + 2 * c + k, (2 * c + k) % MASK_SLOTS, neg_ring[:, c % 2, k * HALF:(k + 1) * HALF, :])
                          for k in range(2)]
                for m, slot, neg in halves:
                    dve.wait_ge(score_ok, m + 1)
                    dve.tensor_tensor(pos_ring[:, slot, :, :], pos_ring[:, slot, :, :], neg, ALU.min)\
                        .then_inc(pos_ok, 1)
                for m, slot, neg in halves:
                    dve.wait_ge(pos_ok, m + 1)
                    dve.tensor_tensor(neg, neg, pos_ring[:, slot, :, :], ALU.subtract).then_inc(mask_ok, 1)

            def split_factors(c):
                js = slice(c * UNIT, (c + 1) * UNIT)
                for k, col in enumerate((e_col, f_col)):
                    if c:
                        dve.wait_ge(factors_ok, 2 * c - 1 + k)
                    dve.tensor_tensor(product[:, k, :, :], wh[:, js, :],
                                      col[:, js].unsqueeze(2).to_broadcast([P, UNIT, F]), ALU.mult)\
                        .then_inc(product_ok, 1)
                for k in range(2):
                    dve.wait_ge(high_ok, 2 * c + k + 1)
                    dve.tensor_tensor(factors[:, k, js, FD:FD + F], product[:, k, :, :], factors[:, k, js, 0:F],
                                      ALU.subtract).then_inc(factors_ok, 1)

            def finish_sums(g):
                for b in range(TPG):
                    dve.wait_ge(pos_copied, TPG * g + b + 1)
                    if b == 0:
                        dve.wait_ge(acc_done, 3 * g + 2)
                    else:
                        dve.wait_ge(mask_used, 8 * (g + 1) + MASK_SLOTS)
                    dve.scalar_tensor_tensor(out=row_sums[:, b, :], in0=acc[2 * b + 1][:, 0:ROW],
                                             scalar=v_col[:, bass.ds(TPG * g + b, 1)], in1=part_sums[:, b, :],
                                             op0=ALU.mult, op1=ALU.add).then_inc(neg_added, 1)
                dve.wait_ge(neg_added, TPG * (g + 1))
                dve.tensor_tensor(nd, nd, row_sums[:, :, FD:ROW], ALU.add).then_inc(nd_ok, 1)
                dve.wait_ge(nd_ok, g + 1)
                dve.tensor_scalar(flag, row_sums[:, :, F], 0.0, None, ALU.is_equal).then_inc(flag_ok, 1)
                dve.wait_ge(flag_ok, g + 1)
                for b in range(TPG):
                    dve.scalar_tensor_tensor(out=nd[:, b, :], in0=mean_row[:, :], scalar=flag[:, b:b + 1],
                                             in1=nd[:, b, :], op0=ALU.mult, op1=ALU.add).then_inc(full_ok, 1)
                dve.wait_ge(full_ok, TPG * (g + 1))
                dve.reciprocal(inv_den, row_sums[:, :, F]).then_inc(inv_den_ok, 1)
                dve.wait_ge(inv_den_ok, g + 1)
                for b in range(TPG):
                    dve.tensor_scalar(hidden[:, b, :], hidden[:, b, :], inv_den[:, b:b + 1], wh_one,
                                      ALU.mult, ALU.mult).then_inc(hidden_ok, 1)
                dve.wait_ge(hidden_ok, TPG * (g + 1))
                dve.tensor_scalar(exp_in, hidden, 0.0, None, ALU.min).then_inc(exp_in_ok, 1)

            def residual(g, first=False):
                dve.wait_ge(exp_ok, g + 1)
                dve.scalar_tensor_tensor(out=hidden, in0=hidden, scalar=0.0, in1=exp_in, op0=ALU.max, op1=ALU.add)\
                    .then_inc(elu_ok, 1)
                dve.wait_ge(elu_ok, g + 1)
                dve.wait_ge(rows_in, 16 * (g + 1))
                if not first:
                    dve.wait_ge(x1_out, 16 * g)
                dve.scalar_tensor_tensor(out=rows_y[:, :, :], in0=hidden, scalar=-1.0, in1=rows_x[:, :, :],
                                         op0=ALU.add, op1=ALU.add).then_inc(y_ok, 1)
                dve.wait_ge(y_ok, g + 1)
                statistics(g, stats_ok, mv_ok)

            def statistics(g, stats_sem, mv_sem):
                for b in range(TPG):
                    dve.bn_stats(stats[:, b, :], rows_y[:, b, :]).then_inc(stats_sem, 1)
                dve.wait_ge(ones_ok, 1)
                dve.wait_ge(stats_sem, TPG * (g + 1))
                for b in range(TPG):
                    dve.bn_aggr(mv[:, b, :], stats[:, b, :]).then_inc(mv_sem, 1)

            def normalise(g, rstd_sem, done):
                dve.wait_ge(rstd_sem, TPG * (g + 1))
                for b in range(TPG):
                    dve.tensor_scalar(rows_y[:, b, :], rows_y[:, b, :], mv[:, b, 0:1], rstd[:, b:b + 1],
                                      ALU.subtract, ALU.mult).then_inc(done, 1)

            def low_parts(g):
                dve.wait_ge(high_part, g + 1)
                dve.scalar_tensor_tensor(out=parts[:, :, FD:FD + F], in0=rows_y[:, :, :], scalar=X_SCALE,
                                         in1=parts[:, :, 0:F], op0=ALU.mult, op1=ALU.subtract).then_inc(low_part, 1)

            def group(g, last=False, second=False):
                for c in range(UPG):
                    masks(g, c, UPG * g + c + 1)
                    if c == 0:
                        finish_sums(g - 1)
                    elif c == 1:
                        residual(g - 1, second)
                    elif c == 3:
                        low_parts(g - 1)

            dve.wait_ge(ef_ok, 2)
            for c in range(UPG):
                split_factors(c)
                masks(0, c, c + 1)
            dve.wait_ge(exp_cols_ok, 4)
            dve.wait_ge(mean_ok, 1)
            dve.wait_ge(one_row_ok, 1)
            group(1, second=True)
            with dve.Fori(2, NG - 1) as g:
                group(g)
            group(NG - 1, last=True)

            def masks_1(g, c):
                dve.wait_ge(mask1_used, UPG * g + c + 1)
                unpack(g, c, ring_1, c).then_inc(mask1_ok, 1)

            def means_1(g, first=False):
                dve.wait_ge(copied1, TPG * (g + 1))
                if not first:
                    dve.wait_ge(turned1, g)
                dve.tensor_tensor(nd, part_sums[:, :, 0:FD], part_sums[:, :, FD:ROW], ALU.add).then_inc(nd1_ok, 1)
                dve.wait_ge(nd1_ok, g + 1)
                dve.reciprocal(inv_den, row_sums[:, :, F]).then_inc(inv1_ok, 1)
                dve.wait_ge(inv1_ok, g + 1)
                for b in range(TPG):
                    dve.tensor_scalar(hidden[:, b, :], hidden[:, b, :], inv_den[:, b:b + 1], 1.0 / X_SCALE,
                                      ALU.mult, ALU.mult).then_inc(mean1_ok, 1)

            def output_1(g, first=False):
                dve.wait_ge(rows1_in, 16 * (g + 1))
                if not first:
                    dve.wait_ge(y_out, 16 * g)
                dve.tensor_tensor(rows_y[:, :, :], rows_x[:, :, :], bias_row[:, :].unsqueeze(1).to_broadcast([P, TPG, F]),
                                  ALU.add).then_inc(xb1_ok, 1)
                dve.wait_ge(xb1_ok, g + 1)
                dve.wait_ge(proj1_ok, g + 1)
                dve.tensor_tensor(rows_y[:, :, :], turn_ps[1][:, 0:TPG * F].rearrange("p (b f) -> p b f", b=TPG),
                                  rows_y[:, :, :], ALU.add).then_inc(y1_ok, 1)
                dve.wait_ge(y1_ok, g + 1)
                statistics(g, stats1_ok, mv1_ok)
                normalise(g, rstd1_ok, out_ok)

            def finish_layer_0():
                finish_sums(NG - 1)
                residual(NG - 1)
                low_parts(NG - 1)

            for c in range(UPG):
                masks_1(0, c)
            finish_layer_0()
            dve.wait_ge(bias_in, 16)
            dve.wait_ge(x1_out, 16 * NG)

            def group_1(g, first=False):
                for c in range(UPG - 1):
                    masks_1(g, c)
                means_1(g - 1, first)
                masks_1(g, UPG - 1)
                output_1(g - 1, first)

            group_1(1, first=True)
            with dve.Fori(2, NG) as g:
                group_1(g)
            means_1(NG - 1)
            output_1(NG - 1)


def kernel(x, adj, L0_gnn_W, L0_gnn_a, L1_gnn_weight, L1_gnn_bias):
    import numpy as _np
    import concourse.bacc as _bacc
    from concourse import mybir as _mybir
    from concourse.bass_utils import run_bass_kernel_spmd as _run

    consts = _np.zeros((P, P + WPT), _np.float32)
    consts[:, :P] = _np.eye(P)
    for p in range(P):
        consts[p, P + p % WPT] = 2.0 ** (p // WPT) / F8_ONE

    nc = _bacc.Bacc("TRN2", target_bir_lowering=False, num_devices=1)
    arrays, args = {}, []
    for name, a in (("x", x), ("adj", adj), ("w0", L0_gnn_W), ("a0", L0_gnn_a), ("w1", L1_gnn_weight),
                    ("b1", L1_gnn_bias), ("consts", consts)):
        a = _np.ascontiguousarray(a)
        arrays[f"in_{name}"] = a
        args.append(nc.dram_tensor(f"in_{name}", a.shape, _mybir.dt.from_np(a.dtype), kind="ExternalInput").ap())
    args.append(nc.dram_tensor("out_0", x.shape, _mybir.dt.float32, kind="ExternalOutput").ap())
    adj_resnorm_kernel(nc, *args)
    r = _run(nc, [arrays], core_ids=[0])
    return r.results[0]["out_0"]
```

```python
from contextlib import ExitStack

import concourse.bass as bass
from concourse import mybir

ALU = mybir.AluOpType
ACT = mybir.ActivationFunctionType
AX = mybir.AxisListType
F32 = mybir.dt.float32
BF16 = mybir.dt.bfloat16
F16 = mybir.dt.float16
F8 = mybir.dt.float8e4
U16 = mybir.dt.uint16
I32 = mybir.dt.int32

P = 128
BITS = 16
WPT = P // BITS
TPG = 2
GROUP = TPG * P
WPG = TPG * WPT
UNIT = 16
HALF = 8
MASK_SLOTS = 4
BIG = 2.0 ** 80
X_SCALE = 2.0 ** 11
E_SCALE = 2.0 ** 14
F8_ONE = 2.0 ** -9
WIDEST = 10.0
MASKED = 9e15
ADJ_SLOTS = 2
RING_1 = 4
EPS = 1e-5
ALPHA = 0.2


def adj_resnorm_kernel(nc, x, adj, w0, a0, w1, b1, consts, out):
    N, F = x.shape
    NG = N // GROUP
    NJ = N // P
    UPG = NJ // UNIT
    FD = F + 1
    ROW = 2 * FD
    XB = 4
    NX = NJ // XB
    X_SLOTS = 4
    COLS = UNIT * P
    WPU = UNIT * WPG

    s_dram = nc.dram_tensor("s_and_t", [2 * NJ, P], F32, kind="Internal").ap()
    wh_dram = nc.dram_tensor("wh_rows", [N, F], F32, kind="Internal").ap()
    x1_dram = nc.dram_tensor("x1_rows", [N, F], F32, kind="Internal").ap()
    parts_dram = nc.dram_tensor("x1_parts", [N, ROW], F16, kind="Internal").ap()

    ctx = ExitStack()
    with ctx:
        def sb(name, shape, dt):
            return ctx.enter_context(nc.sbuf_tensor(name, shape, dt))

        def sem(name):
            return ctx.enter_context(nc.semaphore(name))

        words = sb("words", [P, NG, NJ * WPG], U16)
        factors = sb("factors", [P, 2, NJ, ROW], F16)
        adj_ring = sb("adj_ring", [P, ADJ_SLOTS, TPG, COLS], I32)
        neg_ring = sb("neg_ring", [P, 2, UNIT, GROUP], BF16)
        pos_ring = sb("pos_ring", [P, MASK_SLOTS, HALF, GROUP], BF16)
        consts_sb = sb("consts_sb", [P, P + WPT], F32)
        pack_w = sb("pack_w", [P, WPT], BF16)
        s_row = sb("s_row", [P, 2, GROUP], F32)
        cols = sb("cols", [P, 12, NJ], F32)
        one = sb("one", [P, 24], F32)
        mean_row = sb("mean_row", [P, FD], F32)
        bias_row = sb("bias_row", [P, F], F32)
        w1_sb = sb("w1_sb", [P, 2, F], F32)
        part_sums = sb("part_sums", [P, TPG, ROW], F32)
        row_sums = sb("row_sums", [P, TPG, ROW], F32)
        rows_x = sb("rows_x", [P, TPG, F], F32)
        rows_y = sb("rows_y", [P, TPG, F], F32)
        parts = sb("parts", [P, TPG, ROW], F16)
        stats = sb("stats", [P, TPG, 6], F32)
        mv = sb("mv", [P, TPG, 2], F32)
        wh_top = sb("wh_top", [P, NX], F32)
        x_sums = sb("x_sums", [P, NX], F32)
        wide_flag = sb("wide_flag", [P, 1], I32)
        top_low = sb("top_low", [P, 4], F32)
        wide_one = sb("wide_one", [P, 8], F32)

        ident = consts_sb[:, 0:P]
        s_col, t_col, t_big, e_col, f_col, u_col, v_col, y_col, uy_col, vy_col, e_den, f_den = \
            (cols[:, k, :] for k in range(12))
        t_max, _, wh_max, wh_one, neg_t, neg_ft, inv_wh, scale_e, ones, sum_x = (one[:, k:k + 1] for k in range(10))
        t_max, t_spread = top_low[:, 2:3], wide_one[:, 7:8]
        half_max, row_max, neg_max, half_sum, row_sum = (wide_one[:, a:b] for a, b in ((0, 2), (2, 3), (3, 4), (4, 6), (6, 7)))
        minus_half, inv_den, flag, var_eps, rstd, minus_mean, shift = (one[:, k:k + 2] for k in range(10, 24, 2))
        nd = row_sums[:, :, 0:FD]
        hidden = row_sums[:, :, 0:F]
        exp_in = part_sums[:, :, 0:F]

        wh = words[:, NG // 2:, :].rearrange("p g w -> p (g w)").bitcast(F32)[:, 0:NJ * F]\
            .rearrange("p (j f) -> p j f", f=F)
        early = words[:, 2:NG // 2, :].rearrange("p g w -> p (g w)").bitcast(F32)
        sizes, at, early_of = dict(product=2 * UNIT * F, x_t=2 * XB * F, wq=F + 2, w_turn=P, a_sb=2,
                                   s_turn=P, sum_xb=P), 0, {}
        for name, size in sizes.items():
            early_of[name] = early[:, at:at + size]
            at += size
        product = early_of["product"].rearrange("p (k j f) -> p k j f", k=2, f=F)
        x_in = factors[:, 1, :, :].rearrange("p j r -> p (j r)").bitcast(F32)[:, 0:X_SLOTS * XB * F]\
            .rearrange("p (k j f) -> p k j f", k=X_SLOTS, f=F)
        x_t = early_of["x_t"].rearrange("p (k n) -> p k n", k=2)
        wq, w_turn, a_sb, s_turn, sum_xb = (early_of[n] for n in ("wq", "w_turn", "a_sb", "s_turn", "sum_xb"))
        ring_1 = adj_ring[:, :, :, :].rearrange("p s t c -> p (s t c)").bitcast(BF16)\
            .rearrange("p (s j r) -> p s j r", s=RING_1, j=UNIT)
        turned = pos_ring[:, 0, :, :].rearrange("p j r -> p (j r)").bitcast(F32)[:, 0:2 * TPG * P]

        acc = [ctx.enter_context(nc.psum_tensor(f"acc{k}", [P, 512], F32)) for k in range(2 * TPG)]
        pack_ps = [ctx.enter_context(nc.psum_tensor(f"pack_ps{k}", [P, 512], F32)) for k in range(2)]
        turn_ps = [ctx.enter_context(nc.psum_tensor(f"turn_ps{k}", [P, 512], F32)) for k in range(2)]

        consts_in, w0_in, a0_in, w1_in, bias_in = (sem(n) for n in "consts_in w0_in a0_in w1_in bias_in".split())
        x_in_sem = [sem(f"x_in{k}") for k in range(X_SLOTS)]
        adj_in = [sem("adj_in0"), sem("adj_in1")]
        s_row_in = [sem("s_row_in0"), sem("s_row_in1")]
        rows_in, rows1_in = sem("rows_in"), sem("rows1_in")
        parts_in = [sem(f"parts_in{k}") for k in range(NJ // HALF)]
        s_out, x1_out, parts_out, y_out = (sem(n) for n in "s_out x1_out parts_out y_out".split())
        pack_w_ok, ones_ok, half_ok, tail_ok = (sem(n) for n in "pack_w_ok ones_ok half_ok tail_ok".split())
        w0_turned, w_turn_ok, wa_made, wa_ok = (sem(n) for n in "w0_turned w_turn_ok wa_made wa_ok".split())
        x_turned, x_t_ok, wh_made, wh_ok, top_ok = (sem(n) for n in "x_turned x_t_ok wh_made wh_ok top_ok".split())
        s_turned, s_turn_ok, sum_x_ok, sum_xb_ok = (sem(n) for n in "s_turned s_turn_ok sum_x_ok sum_xb_ok".split())
        mean_made, mean_ok, one_row_ok = (sem(n) for n in "mean_made mean_ok one_row_ok".split())
        t_top_ok, t_max_ok, wh_one_ok, wh_max_ok = (sem(n) for n in "t_top_ok t_max_ok wh_one_ok wh_max_ok".split())
        neg_ok, y_ok_col, uy_ok, exp_cols_ok, t_big_ok = (sem(n) for n in "neg_ok y_col_ok uy_ok exp_cols_ok t_big_ok".split())
        guard_ok, inv_ok, scale_ok, den_ok, den_hi_ok = (sem(n) for n in "guard_ok inv_ok scale_ok den_ok den_hi_ok".split())
        ef_ok, product_ok, high_ok, factors_ok = (sem(n) for n in "ef_ok product_ok high_ok factors_ok".split())
        packed, words_ok, unpacked = (sem(n) for n in "packed words_ok unpacked".split())
        score_ok, pos_ok, mask_ok, mask_used, acc_done = (sem(n) for n in "score_ok pos_ok mask_ok mask_used acc_done".split())
        pos_copied, neg_added, nd_ok, flag_ok, full_ok, inv_den_ok, hidden_ok, exp_in_ok, exp_ok, elu_ok = (
            sem(n) for n in "pos_copied neg_added nd_ok flag_ok full_ok inv_den_ok hidden_ok exp_in_ok exp_ok elu_ok".split())
        y_ok, stats_ok, mv_ok, var_ok, rstd_ok, minus_ok, shift_ok, x1_ok, high_part, low_part = (
            sem(n) for n in "y_ok stats_ok mv_ok var_ok rstd_ok minus_ok shift_ok x1_ok high_part low_part".split())
        (low_ok, spread_ok, wide_ok, wh_saved, wh_out, w_t_in, w_wh_in, w_adj_in, w_x_in, w_stored, w_parts_in, w_step,
         w_max, w_exp, w_turned, w_copied, w_sum, w_hidden, w_elu_in, w_elu, w_y, w_stats, w_mv, w_var, w_rstd, w_x1, w_high,
         w_low, w_masks) = (sem(n) for n in (
            "low_ok spread_ok wide_ok wh_saved wh_out w_t_in w_wh_in w_adj_in w_x_in w_stored w_parts_in w_step "
            "w_max w_exp w_turned w_copied w_sum w_hidden w_elu_in w_elu w_y w_stats w_mv w_var w_rstd w_x1 w_high "
            "w_low w_masks").split())
        mask1_ok, mask1_used, acc1_done, copied1, nd1_ok, inv1_ok, mean1_ok, turned1, turned1_ok, proj1_ok, xb1_ok = (
            sem(n) for n in ("mask1_ok mask1_used acc1_done copied1 nd1_ok inv1_ok mean1_ok turned1 turned1_ok "
                             "proj1_ok xb1_ok").split())
        y1_ok, stats1_ok, mv1_ok, var1_ok, rstd1_ok, out_ok = (
            sem(n) for n in "y1_ok stats1_ok mv1_ok var1_ok rstd1_ok out_ok".split())

        x_tiles = x.rearrange("(j p) f -> p j f", p=P)
        adj_tiles = adj.rearrange("(g k t w) c -> g t k w c", g=NG, k=BITS, t=TPG)
        out_rows = out.rearrange("(g b p) f -> g p b f", g=NG, p=P)
        x_rows = x.rearrange("(g b p) f -> g p b f", g=NG, p=P)
        x1_rows = x1_dram.rearrange("(g b p) f -> g p b f", g=NG, p=P)
        parts_rows = parts_dram.rearrange("(g b p) f -> g p b f", g=NG, p=P)
        parts_tiles = parts_dram.rearrange("(j p) f -> p j f", p=P)
        s_rows = s_dram[0:NJ, :].rearrange("(g j) p -> g (j p)", g=NG)
        t_row_dram = s_dram[NJ:2 * NJ, :].rearrange("j p -> (j p)")
        adj_rows = adj.rearrange("(i p) c -> i p c", p=P)
        x_tile, x1_tile, parts_tile = (d.rearrange("(i p) f -> i p f", p=P) for d in (x, x1_dram, parts_dram))
        wide_f32 = factors[:, :, :, :].rearrange("p k j r -> p (k j r)").bitcast(F32)
        t_all = wide_f32[:, 0:N]
        wh_all = wide_f32[:, N:N + NJ * F].rearrange("p (j f) -> p j f", f=F)
        adj_all = adj_ring[:, :, :, :].rearrange("p s t c -> p (s t c)")
        adj_01 = adj_all.bitcast(F32)
        prob = [r[:, :, :, :].rearrange("p a j r -> p (a j r)").bitcast(F32) for r in (neg_ring, pos_ring)]
        prob_t = [s_row[:, :, :].rearrange("p k r -> p (k r)"),
                  part_sums[:, :, :].rearrange("p b r -> p (b r)")[:, 0:4 * P]]
        HC = N // 2

        def is_wide(eng):
            eng.wait_ge(wide_ok, 1)
            return eng.value_load(wide_flag[0:1, 0:1], min_val=0, max_val=1)

        block = ctx.enter_context(nc.Block())

        @block.sync
        def _(sp):
            def load_adj(g, c):
                sp.wait_ge(packed, UPG * g + c + 1)
                for t in range(TPG):
                    sp.dma_start(adj_ring[:, c % ADJ_SLOTS, t, :],
                                 adj_tiles[g, t, :, :, c * COLS:(c + 1) * COLS])\
                        .then_inc(adj_in[c % ADJ_SLOTS], 16)

            def load_s(g, slot):
                sp.dma_start(s_row[:, slot, :], s_rows[g, :].partition_broadcast(P)).then_inc(s_row_in[slot], 16)

            def store_x1(g):
                sp.wait_ge(x1_ok, TPG * (g + 1))
                sp.dma_start(x1_rows[g], rows_y[:, :, :]).then_inc(x1_out, 16)
                sp.wait_ge(low_part, g + 1)
                sp.dma_start(parts_rows[g], parts[:, :, :]).then_inc(parts_out, 16)

            def load_x(g, first=False):
                if not first:
                    sp.wait_ge(y_ok, g)
                sp.dma_start(rows_x[:, :, :], x_rows[g]).then_inc(rows_in, 16)

            sp.sem_inc(packed, ADJ_SLOTS)
            sp.dma_start(consts_sb[:, :], consts).then_inc(consts_in, 16)
            sp.dma_start(wq[:, 0:F], w0).then_inc(w0_in, 16)
            sp.dma_start(a_sb, a0.rearrange("(k f) o -> f (k o)", k=2), allow_slow_non_contiguous=True).then_inc(a0_in, 16)
            for k in range(X_SLOTS):
                sp.dma_start(x_in[:, k], x_tiles[:, XB * k:XB * (k + 1), :]).then_inc(x_in_sem[k], 16)
            load_adj(0, 0)
            with sp.Fori(1, NX // X_SLOTS) as n:
                for k in range(X_SLOTS):
                    sp.wait_ge(x_turned, X_SLOTS * (n - 1) + k + 1)
                    sp.dma_start(x_in[:, k], x_tiles[:, bass.ds(XB * (X_SLOTS * n + k), XB), :])\
                        .then_inc(x_in_sem[k], 16)
            load_adj(0, 1)
            load_adj(0, 2)
            sp.dma_start(w1_sb[:, :, :], w1.rearrange("(k f) o -> f k o", k=2)).then_inc(w1_in, 16)
            sp.dma_start(bias_row[:, :], b1.partition_broadcast(P)).then_inc(bias_in, 16)
            sp.wait_ge(s_turn_ok, 1)
            sp.dma_start(s_dram, s_turn).then_inc(s_out, 16)
            sp.wait_ge(s_out, 16)
            load_s(0, 0)
            load_s(1, 1)
            load_adj(0, 3)
            load_x(0, True)
            wide = is_wide(sp)
            with sp.If(wide > 0):
                sp.dma_start(wh_dram.rearrange("(j p) f -> p j f", p=P), wh).then_inc(wh_out, 16)
                sp.wait_ge(wh_out, 16)
            sp.sem_inc(wh_saved, 1)

            def group(g, slot, first=False, adj_next=True, s_next=True):
                if adj_next:
                    for c in range(UPG):
                        load_adj(g + 1, c)
                if not first:
                    store_x1(g - 1)
                    load_x(g)
                if s_next:
                    sp.wait_ge(score_ok, 8 * (g + 1))
                    load_s(g + 2, slot)

            group(0, 0, first=True)
            with sp.Fori(0, NG // 2 - 2) as n:
                group(2 * n + 1, 1)
                group(2 * n + 2, 0)
            group(NG - 3, 1)
            group(NG - 2, 0, s_next=False)
            group(NG - 1, 1, adj_next=False, s_next=False)

            sp.wait_ge(mask_used, 8 * NG + MASK_SLOTS)
            sp.wait_ge(parts_out, 16 * (NG - 1))
            for k in range(NJ // HALF):
                if k == NJ // HALF - 1:
                    store_x1(NG - 1)
                    sp.wait_ge(parts_out, 16 * NG)
                sp.dma_start(factors[:, 0, HALF * k:HALF * (k + 1), :], parts_tiles[:, HALF * k:HALF * (k + 1), :])\
                    .then_inc(parts_in[k], 16)
            sp.wait_ge(x1_out, 16 * NG)

            def wide_loads(i):
                sp.wait_ge(w_max, i + 1)
                sp.dma_start(adj_all, adj_rows[i]).then_inc(w_adj_in, 16)
                sp.wait_ge(w_y, i + 1)
                sp.dma_start(rows_x[:, 0, :], x_tile[i]).then_inc(w_x_in, 16)

            with sp.If(wide > 0):
                for k in range(NJ // HALF):
                    sp.wait_ge(parts_in[k], 16)
                sp.wait_ge(mask1_ok, UPG)
                sp.sem_inc(w_max, 1)
                sp.sem_inc(w_y, 1)
                sp.sem_inc(w_stored, 32)
                sp.dma_start(t_all, t_row_dram.partition_broadcast(P)).then_inc(w_t_in, 16)
                sp.dma_start(wh_all, wh_dram.rearrange("(j p) f -> p j f", p=P)).then_inc(w_wh_in, 16)
                with sp.Fori(0, NJ) as i:
                    wide_loads(i)
                    sp.wait_ge(w_x1, i + 1)
                    sp.dma_start(x1_tile[i], rows_y[:, 0, :]).then_inc(w_stored, 16)
                    sp.wait_ge(w_low, i + 1)
                    sp.dma_start(parts_tile[i], parts[:, 0, :]).then_inc(w_stored, 16)
                sp.wait_ge(w_stored, 32 * (NJ + 1))
                sp.dma_start(factors[:, 0, :, :], parts_tiles).then_inc(w_parts_in, 16)

            def rows_1(g):
                sp.dma_start(rows_x[:, :, :], x1_rows[g]).then_inc(rows1_in, 16)

            def store_1(g):
                sp.wait_ge(out_ok, TPG * (g + 1))
                sp.dma_start(out_rows[g], rows_y[:, :, :]).then_inc(y_out, 16)

            rows_1(0)
            with sp.Fori(1, NG) as g:
                sp.wait_ge(turned1, g)
                sp.wait_ge(xb1_ok, g)
                rows_1(g)
                store_1(g - 1)
            store_1(NG - 1)
            sp.wait_ge(y_out, 16 * NG)

        @block.gpsimd
        def _(pool):
            pool.memset(minus_half, -0.5).then_inc(half_ok, 1)
            pool.wait_ge(t_top_ok, 1)
            pool.wait_ge(low_ok, 2)
            pool.partition_all_reduce(top_low[:, 2:4], top_low[:, 0:2], P, bass.bass_isa.ReduceOp.max).then_inc(t_max_ok, 1)
            pool.wait_ge(wh_one_ok, 1)
            pool.partition_all_reduce(wh_max, wh_one, P, bass.bass_isa.ReduceOp.max).then_inc(wh_max_ok, 1)

            pool.wait_ge(ef_ok, 2)
            for c in range(UPG):
                js = slice(c * UNIT, (c + 1) * UNIT)
                for k, col in enumerate((e_col, f_col)):
                    if c:
                        pool.wait_ge(factors_ok, 2 * c - 1 + k)
                    pool.tensor_tensor(product[:, k, :, :], wh[:, js, :],
                                       col[:, js].unsqueeze(2).to_broadcast([P, UNIT, F]), ALU.mult)\
                        .then_inc(product_ok, 1)

            def inverse_deviation(n, mv_sem, var_sem, rstd_sem):
                pool.wait_ge(half_ok, 1)
                pool.wait_ge(mv_sem, n)
                pool.tensor_scalar(var_eps, mv[:, :, 1], EPS, None, ALU.add).then_inc(var_sem, TPG)
                pool.wait_ge(var_sem, n)
                pool.tensor_tensor(rstd, var_eps, minus_half, ALU.pow).then_inc(rstd_sem, TPG)

            with pool.Fori(TPG, TPG * NG + 1, TPG) as n:
                inverse_deviation(n, mv_ok, var_ok, rstd_ok)
                pool.tensor_scalar(minus_mean, mv[:, :, 0], -1.0, None, ALU.mult).then_inc(minus_ok, TPG)
                pool.wait_ge(minus_ok, n)
                pool.wait_ge(rstd_ok, n)
                pool.tensor_tensor(shift, minus_mean, rstd, ALU.mult).then_inc(shift_ok, TPG)
            with pool.If(is_wide(pool) > 0):
                with pool.Fori(TPG, TPG * NJ + 1, TPG) as n:
                    inverse_deviation(n, w_mv, w_var, w_rstd)
            with pool.Fori(TPG, TPG * NG + 1, TPG) as n:
                inverse_deviation(n, mv1_ok, var1_ok, rstd1_ok)

        @block.scalar
        def _(act):
            act.wait_ge(consts_in, 16)
            act.activation(pack_w[:, :], consts_sb[:, P:P + WPT], ACT.Copy).then_inc(pack_w_ok, 1)
            act.wait_ge(w0_turned, 1)
            act.activation(w_turn, turn_ps[0][:, 0:P], ACT.Copy).then_inc(w_turn_ok, 1)
            act.wait_ge(wa_made, 1)
            act.activation(wq[:, F:F + 2], turn_ps[1][:, 0:2], ACT.Copy).then_inc(wa_ok, 1)

            def copy_turned(n, first=False):
                for k in range(2):
                    act.wait_ge(x_turned, 2 * n + k + 1)
                    if not first:
                        act.wait_ge(wh_made, 2 * n + k - 1)
                    act.activation(x_t[:, k, :], turn_ps[k][:, :], ACT.Copy,
                                   accum_out=x_sums[:, bass.ds(2 * n + k, 1)]).then_inc(x_t_ok, 1)

            def copy_words(g, c):
                act.wait_ge(packed, UPG * g + c + 1 + ADJ_SLOTS)
                act.activation(words[:, g, c * WPU:(c + 1) * WPU], pack_ps[c % 2][:, 0:WPU], ACT.Copy)\
                    .then_inc(words_ok, 1)

            copy_turned(0, True)
            with act.Fori(1, NX // 2) as n:
                copy_turned(n)
            act.wait_ge(s_turned, 1)
            act.activation(s_turn, turn_ps[0][:, 0:P], ACT.Copy).then_inc(s_turn_ok, 1)
            copy_words(0, 0)
            copy_words(0, 1)

            act.wait_ge(neg_ok, 2)
            act.activation(e_col, t_col, ACT.Exp, bias=neg_t).then_inc(exp_cols_ok, 1)
            act.activation(f_col, t_col, ACT.Exp, bias=neg_ft, scale=ALPHA).then_inc(exp_cols_ok, 1)
            act.wait_ge(uy_ok, 2)
            act.activation(u_col, uy_col, ACT.Exp).then_inc(exp_cols_ok, 1)
            act.activation(v_col, vy_col, ACT.Exp).then_inc(exp_cols_ok, 1)
            act.wait_ge(t_big_ok, 1)

            def scores(g, slot, h):
                act.wait_ge(mask_used, 8 * g + h + 1)
                for j in range(HALF):
                    a = act.activation(pos_ring[:, h % MASK_SLOTS, j, :], s_row[:, slot, :], ACT.Relu,
                                       bias=t_big[:, h * HALF + j:h * HALF + j + 1], scale=BIG)
                a.then_inc(score_ok, 1)

            def copy_positive(g, first=False):
                if not first:
                    act.wait_ge(elu_ok, g)
                for b in range(TPG):
                    act.wait_ge(acc_done, 3 * g + 2 * b + 1)
                    act.activation(part_sums[:, b, :], acc[2 * b][:, 0:ROW], ACT.Copy,
                                   scale=u_col[:, bass.ds(TPG * g + b, 1)]).then_inc(pos_copied, 1)

            def exponential(g):
                act.wait_ge(exp_in_ok, g + 1)
                act.activation(exp_in, exp_in, ACT.Exp).then_inc(exp_ok, 1)

            def high_parts(g, first=False):
                act.wait_ge(x1_ok, TPG * (g + 1))
                if first:
                    act.wait_ge(tail_ok, 2)
                else:
                    act.wait_ge(parts_out, 16 * g)
                act.activation(parts[:, :, 0:F], rows_y[:, :, :], ACT.Copy, scale=X_SCALE).then_inc(high_part, 1)

            def next_words(g, c, last=False):
                if not (last and c >= 2):
                    copy_words(g + c // 2, (c + 2) % UPG)

            def normalise(g, first=False):
                act.wait_ge(shift_ok, TPG * (g + 1))
                if not first:
                    act.wait_ge(low_part, g)
                for b in range(TPG):
                    act.activation(rows_y[:, b, :], rows_y[:, b, :], ACT.Identity, bias=shift[:, b:b + 1],
                                   scale=rstd[:, b:b + 1]).then_inc(x1_ok, 1)

            def group(g, slot, loads, second=False, last=False):
                act.wait_ge(s_row_in[slot], 16 * loads)
                for h in range(8):
                    scores(g, slot, h)
                    if h % 2:
                        next_words(g, h // 2, last)
                    if h == 2:
                        copy_positive(g - 1, second)
                    if h == 4:
                        exponential(g - 1)
                    if h == 6:
                        normalise(g - 1, second)
                    if h == 7:
                        high_parts(g - 1, second)

            act.wait_ge(s_row_in[0], 16)
            for c in range(UPG):
                for h in (2 * c, 2 * c + 1):
                    scores(0, 0, h)
                for k in range(2):
                    act.wait_ge(product_ok, 2 * c + k + 1)
                    act.activation(factors[:, k, c * UNIT:(c + 1) * UNIT, 0:F], product[:, k, :, :], ACT.Copy)\
                        .then_inc(high_ok, 1)
                next_words(0, c)
            act.wait_ge(wh_saved, 1)
            act.wait_ge(factors_ok, 2 * UPG)
            group(1, 1, 1, second=True)
            with act.Fori(1, NG // 2 - 1) as n:
                group(2 * n, 0, n + 1)
                group(2 * n + 1, 1, n + 1)
            group(NG - 2, 0, NG // 2)
            group(NG - 1, 1, NG // 2, last=True)
            copy_positive(NG - 1)
            exponential(NG - 1)
            normalise(NG - 1)
            high_parts(NG - 1)

            with act.If(is_wide(act) > 0):
                with act.Fori(0, NJ) as i:
                    act.wait_ge(w_max, i + 2)
                    for k in range(2):
                        act.activation(prob[k], prob[k], ACT.Exp, bias=neg_max, accum_out=half_sum[:, k:k + 1])\
                            .then_inc(w_exp, 1)
                    for q in range(NX):
                        act.wait_ge(w_turned, NX * i + q + 1)
                        act.wait_ge(w_sum, NX * i + q + 1)
                        act.activation(prob_t[q % 2], turn_ps[q % 2][:, :], ACT.Copy).then_inc(w_copied, 1)
                    act.wait_ge(w_elu_in, i + 1)
                    act.activation(mean_row[:, 0:F], mean_row[:, 0:F], ACT.Exp).then_inc(w_elu, 1)
                    act.wait_ge(w_x1, i + 1)
                    act.activation(parts[:, 0, 0:F], rows_y[:, 0, :], ACT.Copy, scale=X_SCALE).then_inc(w_high, 1)

            def copy_sums(g, first=False):
                if first:
                    act.wait_ge(elu_ok, NG)
                else:
                    act.wait_ge(nd1_ok, g)
                act.wait_ge(acc1_done, g + 1)
                act.activation(part_sums[:, 0, :], acc[0][:, 0:ROW], ACT.Copy).then_inc(copied1, 1)
                act.wait_ge(mask1_used, UPG * (g + 1) + RING_1)
                act.activation(part_sums[:, 1, :], acc[1][:, 0:ROW], ACT.Copy).then_inc(copied1, 1)

            def copy_turned_1(g, first=False):
                act.wait_ge(turned1, g + 1)
                if not first:
                    act.wait_ge(proj1_ok, g)
                act.activation(turned, turn_ps[0][:, :], ACT.Copy).then_inc(turned1_ok, 1)

            copy_sums(0, True)
            copy_turned_1(0, True)
            with act.Fori(1, NG) as g:
                copy_sums(g)
                copy_turned_1(g)

        @block.tensor
        def _(pe):
            pe.sem_inc(mask_used, MASK_SLOTS)
            pe.sem_inc(mask1_used, RING_1)
            pe.wait_ge(consts_in, 16)
            pe.wait_ge(w0_in, 16)
            pe.transpose(turn_ps[0][:, 0:P], wq[:, 0:F], ident).then_inc(w0_turned, 1)
            pe.wait_ge(w_turn_ok, 1)
            pe.wait_ge(a0_in, 16)
            pe.matmul(turn_ps[1][:, 0:2], w_turn, a_sb, start=True, stop=True).then_inc(wa_made, 1)
            pe.wait_ge(wa_ok, 1)
            pe.wait_ge(ones_ok, 1)

            def turn_x(n, k, first=False):
                pe.wait_ge(x_in_sem[k], 16 * (n + 1))
                if not first:
                    pe.wait_ge(x_t_ok, X_SLOTS * n + k - 1)
                for j in range(XB):
                    m = pe.transpose(turn_ps[k % 2][:, j * P:(j + 1) * P], x_in[:, k, j, :], ident)
                m.then_inc(x_turned, 1)

            def make_wh(n, k, first=False):
                pe.wait_ge(x_t_ok, X_SLOTS * n + k + 1)
                if not first:
                    pe.wait_ge(wh_ok, X_SLOTS * n + k - 1)
                for j in range(XB):
                    o = (j % 2) * (F + 2)
                    m = pe.matmul(acc[2 * (k % 2) + j // 2][:, o:o + F + 2], x_t[:, k % 2, j * P:(j + 1) * P], wq,
                                  start=True, stop=True)
                m.then_inc(wh_made, 1)

            def wh_steps(n, first=False, last=False):
                for k in range(X_SLOTS):
                    if k + 1 < X_SLOTS:
                        turn_x(n, k + 1, first and k == 0)
                    elif not last:
                        turn_x(n + 1, 0)
                    make_wh(n, k, first and k < 2)

            def packable(g, c, first=False):
                pe.wait_ge(adj_in[c % ADJ_SLOTS], 32 * (UPG // ADJ_SLOTS * g + c // ADJ_SLOTS + 1))
                if not first:
                    pe.wait_ge(words_ok, UPG * g + c - 1)

            def pack(c):
                for j in range(UNIT):
                    for t in range(TPG):
                        o = (j * TPG + t) * WPT
                        low_bytes = adj_ring[:, c % ADJ_SLOTS, t, j * P:(j + 1) * P].bitcast(F8)\
                            .rearrange("p (c b) -> p c b", b=4)[:, :, 0]
                        m = pe.matmul(pack_ps[c % 2][:, o:o + WPT], low_bytes, pack_w[:, :], start=True, stop=True)
                m.then_inc(packed, 1)

            turn_x(0, 0, True)
            wh_steps(0, first=True)
            with pe.Fori(1, NX // X_SLOTS - 1) as n:
                wh_steps(n)
            pe.wait_ge(pack_w_ok, 1)
            packable(0, 0, first=True)
            pack(0)
            wh_steps(NX // X_SLOTS - 1, last=True)
            pe.wait_ge(wh_ok, NX)
            pe.transpose(turn_ps[0][:, 0:P], cols[:, 0:2, :].rearrange("p k j -> p (k j)"), ident).then_inc(s_turned, 1)
            packable(0, 1, first=True)
            pack(1)
            pe.wait_ge(sum_xb_ok, 1)
            pe.matmul(turn_ps[1][:, 0:F], sum_xb, wq[:, 0:F], start=True, stop=True).then_inc(mean_made, 1)
            for c in range(2, UPG):
                packable(0, c)
                pack(c)

            def multiply(g, h, first=False):
                pe.wait_ge(mask_ok, 8 * g + h + 1)
                for a in range(2 * TPG):
                    b, neg = a // 2, a % 2
                    if h == 0 and not first:
                        pe.wait_ge(neg_added if neg else pos_copied, TPG * (g - 1) + b + 1)
                    for j in range(HALF):
                        jj = h * HALF + j
                        mask = neg_ring[:, (h // 2) % 2, (h % 2) * HALF + j, b * P:(b + 1) * P] if neg else \
                            pos_ring[:, h % MASK_SLOTS, j, b * P:(b + 1) * P]
                        m = pe.matmul(acc[a][:, 0:ROW], mask, factors[:, neg, jj, :],
                                      start=(jj == 0), stop=(jj == NJ - 1))
                    if h == 7 and a < 2 * TPG - 1:
                        m.then_inc(acc_done, 1)
                m.then_inc(mask_used, 1)

            def group(g, first=False, last=False):
                for c in range(UPG):
                    for h in (2 * c, 2 * c + 1):
                        if first and h % 2 == 0:
                            pe.wait_ge(factors_ok, 2 * (c + 1))
                        if h % 2 and not last:
                            packable(g + 1, c)
                        multiply(g, h, first)
                    if not last:
                        pack(c)

            pe.wait_ge(den_hi_ok, 4)
            group(0, first=True)
            with pe.Fori(1, NG - 1) as g:
                group(g)
            group(NG - 1, last=True)

            with pe.If(is_wide(pe) > 0):
                pe.sem_inc(w_sum, 2)
                pe.wait_ge(low_part, NG)
                pe.wait_ge(w_wh_in, 16)

                def wide_turn(i, q):
                    pe.wait_ge(w_copied, NX * i + q + 1)
                    for j in range(XB):
                        tile = prob[q // (NX // 2)][:, (XB * (q % (NX // 2)) + j) * P:(XB * (q % (NX // 2)) + j + 1) * P]
                        m = pe.transpose(turn_ps[q % 2][:, j * P:(j + 1) * P], tile, ident)
                    m.then_inc(w_turned, 1)

                pe.sem_inc(w_copied, 2)
                with pe.Fori(0, NJ) as i:
                    pe.wait_ge(w_exp, 2 * i + 2)
                    pe.wait_ge(w_hidden, i + 1)
                    for q in range(NX):
                        wide_turn(i, q)
                        pe.wait_ge(w_copied, NX * i + q + 3)
                        for j in range(XB):
                            m = pe.matmul(acc[0][:, 0:F], prob_t[q % 2][:, j * P:(j + 1) * P], wh_all[:, XB * q + j, :],
                                          start=(q == 0 and j == 0), stop=(q == NX - 1 and j == XB - 1))
                        m.then_inc(w_sum, 1)
                pe.wait_ge(w_parts_in, 16)
                pe.wait_ge(w_masks, UPG)

            def multiply_1(g, c, first=False):
                pe.wait_ge(mask1_ok, UPG * g + c + 1)
                for b in range(TPG):
                    if c == 0 and first:
                        pe.wait_ge(neg_added if b else pos_copied, TPG * (NG - 1) + 1)
                    elif c == 0:
                        pe.wait_ge(copied1, TPG * (g - 1) + b + 1)
                    for j in range(UNIT):
                        jj = c * UNIT + j
                        if first and b == 0 and j % HALF == 0:
                            pe.wait_ge(parts_in[jj // HALF], 16)
                        m = pe.matmul(acc[b][:, 0:ROW], ring_1[:, c, j, b * P:(b + 1) * P], factors[:, 0, jj, :],
                                      start=(jj == 0), stop=(jj == NJ - 1))
                    if c == UPG - 1 and b == 0:
                        m.then_inc(acc1_done, 1)
                m.then_inc(mask1_used, 1)

            def turn_rows(g, first=False):
                pe.wait_ge(mean1_ok, TPG * (g + 1))
                pe.wait_ge(rows1_in, 16 * (g + 1))
                if not first:
                    pe.wait_ge(turned1_ok, g)
                for k, rows in enumerate((hidden, rows_x)):
                    for b in range(TPG):
                        m = pe.transpose(turn_ps[0][:, (TPG * k + b) * P:(TPG * k + b + 1) * P], rows[:, b, :], ident)
                m.then_inc(turned1, 1)

            def project(g, first=False):
                pe.wait_ge(turned1_ok, g + 1)
                if not first:
                    pe.wait_ge(y1_ok, g)
                for b in range(TPG):
                    for k in range(2):
                        m = pe.matmul(turn_ps[1][:, b * F:(b + 1) * F],
                                      turned[:, (TPG * k + b) * P:(TPG * k + b + 1) * P], w1_sb[:, k, :],
                                      start=(k == 0), stop=(k == 1))
                m.then_inc(proj1_ok, 1)

            def group_1(g, first=False, second=False):
                for c in range(UPG):
                    multiply_1(g, c, first)
                    if c == 0 and not first:
                        turn_rows(g - 1, second)
                    if c == 1 and not first:
                        project(g - 1, second)

            pe.wait_ge(w1_in, 16)
            group_1(0, first=True)
            group_1(1, second=True)
            with pe.Fori(2, NG) as g:
                group_1(g)
            turn_rows(NG - 1)
            project(NG - 1)

        @block.vector
        def _(dve):
            dve.memset(ones, 1.0).then_inc(ones_ok, 1)
            dve.memset(mean_row[:, F:FD], 1.0).then_inc(one_row_ok, 1)
            dve.memset(parts[:, :, F:FD], 1.0).then_inc(tail_ok, 1)
            dve.memset(parts[:, :, ROW - 1:ROW], 0.0).then_inc(tail_ok, 1)

            def copy_wh(n, k):
                dve.wait_ge(wh_made, 2 * n + k + 1)
                for half in range(2):
                    bank = acc[2 * k + half][:, 0:2 * (F + 2)].rearrange("p (j f) -> p j f", j=2)
                    j0 = 2 * XB * n + XB * k + 2 * half
                    dve.tensor_copy(wh[:, bass.ds(j0, 2), :], bank[:, :, 0:F])
                    d = dve.tensor_copy(cols[:, 0:2, bass.ds(j0, 2)], bank[:, :, F:F + 2].rearrange("p j k -> p k j"))
                d.then_inc(wh_ok, 1)
                dve.wait_ge(wh_ok, 2 * n + k + 1)
                dve.tensor_reduce(wh_top[:, bass.ds(2 * n + k, 1)], wh[:, bass.ds(2 * XB * n + XB * k, XB), :], AX.XY,
                                  ALU.max, apply_absolute_value=True).then_inc(top_ok, 1)

            with dve.Fori(0, NX // 2) as n:
                for k in range(2):
                    copy_wh(n, k)
            dve.tensor_reduce(top_low[:, 0:1], t_col, AX.X, ALU.max).then_inc(t_top_ok, 1)
            dve.tensor_reduce(top_low[:, 1:2], t_col, AX.X, ALU.min).then_inc(low_ok, 1)
            dve.wait_ge(low_ok, 1)
            dve.tensor_scalar(top_low[:, 1:2], top_low[:, 1:2], -1.0, None, ALU.mult).then_inc(low_ok, 1)
            dve.wait_ge(top_ok, NX)
            dve.tensor_reduce(wh_one, wh_top[:, :], AX.X, ALU.max).then_inc(wh_one_ok, 1)
            dve.tensor_scalar(t_big, t_col, BIG, None, ALU.mult).then_inc(t_big_ok, 1)
            dve.wait_ge(x_t_ok, NX)
            dve.tensor_reduce(sum_x, x_sums[:, :], AX.X, ALU.add).then_inc(sum_x_ok, 1)
            dve.wait_ge(sum_x_ok, 1)
            dve.tensor_scalar(sum_xb, ident, 0.0, sum_x, ALU.mult, ALU.add).then_inc(sum_xb_ok, 1)

            dve.wait_ge(t_max_ok, 1)
            dve.tensor_scalar(neg_t, t_max, -1.0, None, ALU.mult).then_inc(neg_ok, 1)
            dve.tensor_scalar(neg_ft, t_max, -ALPHA, None, ALU.mult).then_inc(neg_ok, 1)
            dve.tensor_scalar(y_col, s_col, t_max, None, ALU.add).then_inc(y_ok_col, 1)
            dve.tensor_scalar(t_spread, t_max, top_low[:, 3:4], None, ALU.add).then_inc(spread_ok, 1)
            dve.wait_ge(spread_ok, 1)
            dve.tensor_scalar(wide_flag[:, :], t_spread, WIDEST, None, ALU.is_gt).then_inc(wide_ok, 1)
            dve.wait_ge(y_ok_col, 1)
            dve.tensor_scalar(uy_col, y_col, 1.0 - ALPHA, 0.0, ALU.mult, ALU.min).then_inc(uy_ok, 1)
            dve.tensor_scalar(vy_col, y_col, ALPHA - 1.0, 0.0, ALU.mult, ALU.min).then_inc(uy_ok, 1)
            dve.wait_ge(wh_max_ok, 1)
            dve.tensor_scalar(wh_one, wh_max, 1e-30, None, ALU.max).then_inc(guard_ok, 1)
            dve.wait_ge(guard_ok, 1)
            dve.reciprocal(inv_wh, wh_one).then_inc(inv_ok, 1)
            dve.wait_ge(inv_ok, 1)
            dve.tensor_scalar(scale_e, inv_wh, E_SCALE, None, ALU.mult).then_inc(scale_ok, 1)
            dve.wait_ge(exp_cols_ok, 2)
            dve.wait_ge(scale_ok, 1)
            for k, (col, den) in enumerate(((e_col, e_den), (f_col, f_den))):
                dve.tensor_scalar(den, col, E_SCALE, None, ALU.mult).then_inc(den_ok, 1)
                dve.wait_ge(den_ok, k + 1)
                dve.tensor_copy(factors[:, k, :, F], den).then_inc(den_hi_ok, 1)
                dve.wait_ge(den_hi_ok, 2 * k + 1)
                dve.tensor_tensor(factors[:, k, :, ROW - 1], den, factors[:, k, :, F], ALU.subtract)\
                    .then_inc(den_hi_ok, 1)
                dve.tensor_scalar(col, col, scale_e, None, ALU.mult).then_inc(ef_ok, 1)

            def unpack(g, c, ring, slot, bits=range(BITS)):
                src = words[:, g, c * WPU:(c + 1) * WPU].rearrange("p (j w) -> p j w", j=UNIT)
                dst = ring[:, slot, :, :].bitcast(U16)
                for k in bits:
                    to = dst[:, :, k * WPG:(k + 1) * WPG]
                    if k < 14:
                        d = dve.tensor_scalar(to, src, 14 - k, 0x4000, ALU.logical_shift_left, ALU.bitwise_and)
                    else:
                        d = dve.tensor_scalar(to, src, k - 14, 0x4000, ALU.logical_shift_right, ALU.bitwise_and)
                return d

            def masks(g, c, output=None, second=False):
                dve.wait_ge(mask_used, 8 * g + 2 * c + 2)
                dve.wait_ge(words_ok, UPG * g + c + 1)
                if output == "sums":
                    add_negative(g - 1)
                elif output == "residual":
                    add_elu(g - 1)
                unpack(g, c, neg_ring, c % 2, range(0, 4))
                if output == "sums":
                    add_parts(g - 1)
                elif output == "residual":
                    add_x(g - 1, second)
                unpack(g, c, neg_ring, c % 2, range(4, 8))
                if output == "sums":
                    find_empty(g - 1)
                elif output == "residual":
                    statistics(g - 1, stats_ok)
                unpack(g, c, neg_ring, c % 2, range(8, 12))
                if output == "sums":
                    fill_empty(g - 1)
                elif output == "residual":
                    aggregate(g - 1, stats_ok, mv_ok)
                unpack(g, c, neg_ring, c % 2, range(12, 16)).then_inc(unpacked, 1)
                if output == "sums":
                    invert_sum(g - 1)
                positive(g, c, 0)
                if output == "sums":
                    divide(g - 1)
                positive(g, c, 1)
                if output == "sums":
                    exp_input(g - 1)
                for k in range(2):
                    dve.wait_ge(pos_ok, 8 * g + 2 * c + k + 1)
                    neg = neg_ring[:, c % 2, k * HALF:(k + 1) * HALF, :]
                    dve.tensor_tensor(neg, neg, pos_ring[:, (2 * c + k) % MASK_SLOTS, :, :], ALU.subtract)\
                        .then_inc(mask_ok, 1)

            def positive(g, c, k):
                dve.wait_ge(unpacked, UPG * g + c + 1)
                dve.wait_ge(score_ok, 8 * g + 2 * c + k + 1)
                pos = pos_ring[:, (2 * c + k) % MASK_SLOTS, :, :]
                dve.tensor_tensor(pos, pos, neg_ring[:, c % 2, k * HALF:(k + 1) * HALF, :], ALU.min).then_inc(pos_ok, 1)

            def split_factors(c):
                js = slice(c * UNIT, (c + 1) * UNIT)
                for k in range(2):
                    dve.wait_ge(high_ok, 2 * c + k + 1)
                    dve.tensor_tensor(factors[:, k, js, FD:FD + F], product[:, k, :, :], factors[:, k, js, 0:F],
                                      ALU.subtract).then_inc(factors_ok, 1)

            def add_negative(g):
                for b in range(TPG):
                    dve.wait_ge(pos_copied, TPG * g + b + 1)
                    if b == 0:
                        dve.wait_ge(acc_done, 3 * g + 2)
                    else:
                        dve.wait_ge(mask_used, 8 * (g + 1) + MASK_SLOTS)
                    dve.scalar_tensor_tensor(out=row_sums[:, b, :], in0=acc[2 * b + 1][:, 0:ROW],
                                             scalar=v_col[:, bass.ds(TPG * g + b, 1)], in1=part_sums[:, b, :],
                                             op0=ALU.mult, op1=ALU.add).then_inc(neg_added, 1)

            def add_parts(g):
                dve.wait_ge(neg_added, TPG * (g + 1))
                dve.tensor_tensor(nd, nd, row_sums[:, :, FD:ROW], ALU.add).then_inc(nd_ok, 1)

            def find_empty(g):
                dve.wait_ge(nd_ok, g + 1)
                dve.tensor_scalar(flag, row_sums[:, :, F], 0.0, None, ALU.is_equal).then_inc(flag_ok, 1)

            def fill_empty(g):
                dve.wait_ge(flag_ok, g + 1)
                for b in range(TPG):
                    dve.scalar_tensor_tensor(out=nd[:, b, :], in0=mean_row[:, :], scalar=flag[:, b:b + 1],
                                             in1=nd[:, b, :], op0=ALU.mult, op1=ALU.add).then_inc(full_ok, 1)

            def invert_sum(g):
                dve.wait_ge(full_ok, TPG * (g + 1))
                dve.reciprocal(inv_den, row_sums[:, :, F]).then_inc(inv_den_ok, 1)

            def divide(g):
                dve.wait_ge(inv_den_ok, g + 1)
                for b in range(TPG):
                    dve.tensor_scalar(hidden[:, b, :], hidden[:, b, :], inv_den[:, b:b + 1], wh_one,
                                      ALU.mult, ALU.mult).then_inc(hidden_ok, 1)

            def exp_input(g):
                dve.wait_ge(hidden_ok, TPG * (g + 1))
                dve.tensor_scalar(exp_in, hidden, 0.0, None, ALU.min).then_inc(exp_in_ok, 1)

            def add_elu(g):
                dve.wait_ge(exp_ok, g + 1)
                dve.scalar_tensor_tensor(out=hidden, in0=hidden, scalar=0.0, in1=exp_in, op0=ALU.max, op1=ALU.add)\
                    .then_inc(elu_ok, 1)

            def add_x(g, first=False):
                dve.wait_ge(elu_ok, g + 1)
                dve.wait_ge(rows_in, 16 * (g + 1))
                if not first:
                    dve.wait_ge(x1_out, 16 * g)
                dve.scalar_tensor_tensor(out=rows_y[:, :, :], in0=hidden, scalar=-1.0, in1=rows_x[:, :, :],
                                         op0=ALU.add, op1=ALU.add).then_inc(y_ok, 1)

            def statistics(g, stats_sem, rows_ok=None):
                dve.wait_ge(y_ok if rows_ok is None else rows_ok, g + 1)
                for b in range(TPG):
                    dve.bn_stats(stats[:, b, :], rows_y[:, b, :]).then_inc(stats_sem, 1)

            def aggregate(g, stats_sem, mv_sem):
                dve.wait_ge(ones_ok, 1)
                dve.wait_ge(stats_sem, TPG * (g + 1))
                for b in range(TPG):
                    dve.bn_aggr(mv[:, b, :], stats[:, b, :]).then_inc(mv_sem, 1)

            def normalise(g, rstd_sem, done):
                dve.wait_ge(rstd_sem, TPG * (g + 1))
                for b in range(TPG):
                    dve.tensor_scalar(rows_y[:, b, :], rows_y[:, b, :], mv[:, b, 0:1], rstd[:, b:b + 1],
                                      ALU.subtract, ALU.mult).then_inc(done, 1)

            def low_parts(g):
                dve.wait_ge(high_part, g + 1)
                dve.scalar_tensor_tensor(out=parts[:, :, FD:FD + F], in0=rows_y[:, :, :], scalar=X_SCALE,
                                         in1=parts[:, :, 0:F], op0=ALU.mult, op1=ALU.subtract).then_inc(low_part, 1)

            def group(g, second=False):
                masks(g, 0)
                masks(g, 1, "sums")
                masks(g, 2, "residual", second)
                masks(g, 3)
                low_parts(g - 1)

            for c in range(UPG):
                masks(0, c)
                split_factors(c)
            dve.wait_ge(mean_made, 1)
            dve.tensor_scalar(mean_row[:, 0:F], turn_ps[1][:, 0:F], 1.0 / N, inv_wh, ALU.mult, ALU.mult)\
                .then_inc(mean_ok, 1)
            dve.wait_ge(exp_cols_ok, 4)
            dve.wait_ge(mean_ok, 1)
            dve.wait_ge(one_row_ok, 1)
            group(1, second=True)
            with dve.Fori(2, NG - 1) as g:
                group(g)
            group(NG - 1)

            def masks_1(g, c):
                dve.wait_ge(mask1_used, UPG * g + c + 1)
                unpack(g, c, ring_1, c).then_inc(mask1_ok, 1)

            def means_1(g, first=False):
                dve.wait_ge(copied1, TPG * (g + 1))
                if not first:
                    dve.wait_ge(turned1, g)
                dve.tensor_tensor(nd, part_sums[:, :, 0:FD], part_sums[:, :, FD:ROW], ALU.add).then_inc(nd1_ok, 1)
                dve.wait_ge(nd1_ok, g + 1)
                dve.reciprocal(inv_den, row_sums[:, :, F]).then_inc(inv1_ok, 1)
                dve.wait_ge(inv1_ok, g + 1)
                for b in range(TPG):
                    dve.tensor_scalar(hidden[:, b, :], hidden[:, b, :], inv_den[:, b:b + 1], 1.0 / X_SCALE,
                                      ALU.mult, ALU.mult).then_inc(mean1_ok, 1)

            def add_bias(g, first=False):
                dve.wait_ge(rows1_in, 16 * (g + 1))
                if not first:
                    dve.wait_ge(y_out, 16 * g)
                dve.tensor_tensor(rows_y[:, :, :], rows_x[:, :, :], bias_row[:, :].unsqueeze(1).to_broadcast([P, TPG, F]),
                                  ALU.add).then_inc(xb1_ok, 1)

            def output_1(g):
                dve.wait_ge(xb1_ok, g + 1)
                dve.wait_ge(proj1_ok, g + 1)
                dve.tensor_tensor(rows_y[:, :, :], turn_ps[1][:, 0:TPG * F].rearrange("p (b f) -> p b f", b=TPG),
                                  rows_y[:, :, :], ALU.add).then_inc(y1_ok, 1)
                statistics(g, stats1_ok, y1_ok)
                aggregate(g, stats1_ok, mv1_ok)
                normalise(g, rstd1_ok, out_ok)

            def finish_layer_0():
                for step in (add_negative, add_parts, find_empty, fill_empty, invert_sum, divide, exp_input, add_elu, add_x):
                    step(NG - 1)
                statistics(NG - 1, stats_ok)
                aggregate(NG - 1, stats_ok, mv_ok)
                low_parts(NG - 1)

            for c in range(UPG):
                masks_1(0, c)
            finish_layer_0()

            def wide_tile(i):
                steps = [0]
                STEPS = 18

                def then(instruction):
                    steps[0] += 1
                    instruction.then_inc(w_step, 1)
                    dve.wait_ge(w_step, STEPS * i + steps[0])

                dve.wait_ge(w_adj_in, 16 * (i + 1))
                dve.wait_ge(w_sum, NX * i + 2)
                for k in range(2):
                    p, c = prob[k], slice(k * HC, (k + 1) * HC)
                    then(dve.tensor_scalar(p, t_all[:, c], cols[:, 0, bass.ds(i, 1)], None, ALU.add))
                    then(dve.scalar_tensor_tensor(out=p, in0=p, scalar=ALPHA, in1=p, op0=ALU.mult, op1=ALU.max))
                    then(dve.tensor_scalar(adj_01[:, c], adj_all[:, c], 0, None, ALU.is_gt))
                    then(dve.tensor_tensor(p, p, adj_01[:, c], ALU.mult))
                    then(dve.tensor_scalar(adj_01[:, c], adj_01[:, c], -1.0, MASKED, ALU.add, ALU.mult))
                    then(dve.tensor_tensor(p, p, adj_01[:, c], ALU.add))
                    then(dve.tensor_reduce(half_max[:, k:k + 1], p, AX.X, ALU.max))
                then(dve.tensor_reduce(row_max, half_max, AX.X, ALU.max))
                dve.tensor_scalar(neg_max, row_max, -1.0, None, ALU.mult).then_inc(w_max, 1)
                dve.wait_ge(w_exp, 2 * i + 2)
                then(dve.tensor_reduce(row_sum, half_sum, AX.X, ALU.add))
                then(dve.reciprocal(row_sum, row_sum))
                dve.wait_ge(w_sum, NX * (i + 1) + 2)
                dve.tensor_scalar(hidden[:, 0, :], acc[0][:, 0:F], row_sum, None, ALU.mult).then_inc(w_hidden, 1)
                dve.wait_ge(w_hidden, i + 2)
                dve.tensor_scalar(mean_row[:, 0:F], hidden[:, 0, :], 0.0, None, ALU.min).then_inc(w_elu_in, 1)
                dve.wait_ge(w_elu, i + 1)
                then(dve.scalar_tensor_tensor(out=hidden[:, 0, :], in0=hidden[:, 0, :], scalar=0.0,
                                              in1=mean_row[:, 0:F], op0=ALU.max, op1=ALU.add))
                dve.wait_ge(w_x_in, 16 * (i + 1))
                dve.wait_ge(w_stored, 32 * i + 32)
                dve.scalar_tensor_tensor(out=rows_y[:, 0, :], in0=hidden[:, 0, :], scalar=-1.0, in1=rows_x[:, 0, :],
                                         op0=ALU.add, op1=ALU.add).then_inc(w_y, 1)
                dve.wait_ge(w_y, i + 2)
                dve.bn_stats(stats[:, 0, :], rows_y[:, 0, :]).then_inc(w_stats, 1)
                dve.wait_ge(ones_ok, 1)
                dve.wait_ge(w_stats, i + 1)
                dve.bn_aggr(mv[:, 0, :], stats[:, 0, :]).then_inc(w_mv, TPG)
                dve.wait_ge(w_rstd, TPG * (i + 1))
                dve.tensor_scalar(rows_y[:, 0, :], rows_y[:, 0, :], mv[:, 0, 0:1], rstd[:, 0:1],
                                  ALU.subtract, ALU.mult).then_inc(w_x1, 1)
                dve.wait_ge(w_x1, i + 1)
                dve.wait_ge(w_high, i + 1)
                dve.scalar_tensor_tensor(out=parts[:, 0, FD:FD + F], in0=rows_y[:, 0, :], scalar=X_SCALE,
                                         in1=parts[:, 0, 0:F], op0=ALU.mult, op1=ALU.subtract).then_inc(w_low, 1)
                assert steps[0] == STEPS

            with dve.If(is_wide(dve) > 0):
                dve.wait_ge(w_t_in, 16)
                dve.sem_inc(w_hidden, 1)
                with dve.Fori(0, NJ) as i:
                    wide_tile(i)
                for c in range(UPG):
                    unpack(0, c, ring_1, c).then_inc(w_masks, 1)

            dve.wait_ge(bias_in, 16)
            dve.wait_ge(x1_out, 16 * NG)

            def group_1(g, first=False):
                for c in range(UPG):
                    if c == UPG // 2:
                        means_1(g - 1, first)
                        add_bias(g - 1, first)
                    masks_1(g, c)
                output_1(g - 1)

            group_1(1, first=True)
            with dve.Fori(2, NG) as g:
                group_1(g)
            means_1(NG - 1)
            add_bias(NG - 1)
            output_1(NG - 1)


def kernel(x, adj, L0_gnn_W, L0_gnn_a, L1_gnn_weight, L1_gnn_bias):
    import numpy as _np
    import concourse.bacc as _bacc
    from concourse import mybir as _mybir
    from concourse.bass_utils import run_bass_kernel_spmd as _run

    consts = _np.zeros((P, P + WPT), _np.float32)
    consts[:, :P] = _np.eye(P)
    for p in range(P):
        consts[p, P + p % WPT] = 2.0 ** (p // WPT) / F8_ONE

    nc = _bacc.Bacc("TRN2", target_bir_lowering=False, num_devices=1)
    arrays, args = {}, []
    for name, a in (("x", x), ("adj", adj), ("w0", L0_gnn_W), ("a0", L0_gnn_a), ("w1", L1_gnn_weight),
                    ("b1", L1_gnn_bias), ("consts", consts)):
        a = _np.ascontiguousarray(a)
        arrays[f"in_{name}"] = a
        args.append(nc.dram_tensor(f"in_{name}", a.shape, _mybir.dt.from_np(a.dtype), kind="ExternalInput").ap())
    args.append(nc.dram_tensor("out_0", x.shape, _mybir.dt.float32, kind="ExternalOutput").ap())
    adj_resnorm_kernel(nc, *args)
    r = _run(nc, [arrays], core_ids=[0])
    return r.results[0]["out_0"]
```

```python
from contextlib import ExitStack

import concourse.bass as bass
from concourse import mybir

ALU = mybir.AluOpType
ACT = mybir.ActivationFunctionType
AX = mybir.AxisListType
F32 = mybir.dt.float32
BF16 = mybir.dt.bfloat16
F16 = mybir.dt.float16
F8 = mybir.dt.float8e4
U16 = mybir.dt.uint16
I32 = mybir.dt.int32

P = 128
BITS = 16
WPT = P // BITS
TPG = 2
GROUP = TPG * P
WPG = TPG * WPT
UNIT = 16
HALF = 8
MASK_SLOTS = 4
BIG = 2.0 ** 80
X_SCALE = 2.0 ** 11
E_SCALE = 2.0 ** 14
F8_ONE = 2.0 ** -9
WIDEST = 10.0
MASKED = 9e15
ADJ_SLOTS = 2
RING_1 = 4
EPS = 1e-5
ALPHA = 0.2


def adj_resnorm_kernel(nc, x, adj, w0, a0, w1, b1, consts, out):
    N, F = x.shape
    NG = N // GROUP
    NJ = N // P
    UPG = NJ // UNIT
    FD = F + 1
    ROW = 2 * FD
    XB = 4
    NX = NJ // XB
    X_SLOTS = 4
    COLS = UNIT * P
    WPU = UNIT * WPG

    s_dram = nc.dram_tensor("s_and_t", [2 * NJ, P], F32, kind="Internal").ap()
    wh_dram = nc.dram_tensor("wh_rows", [N, F], F32, kind="Internal").ap()
    x1_dram = nc.dram_tensor("x1_rows", [N, F], F32, kind="Internal").ap()
    parts_dram = nc.dram_tensor("x1_parts", [N, ROW], F16, kind="Internal").ap()

    ctx = ExitStack()
    with ctx:
        def sb(name, shape, dt):
            return ctx.enter_context(nc.sbuf_tensor(name, shape, dt))

        def sem(name):
            return ctx.enter_context(nc.semaphore(name))

        words = sb("words", [P, NG, NJ * WPG], U16)
        factors = sb("factors", [P, 2, NJ, ROW], F16)
        adj_ring = sb("adj_ring", [P, ADJ_SLOTS, TPG, COLS], I32)
        neg_ring = sb("neg_ring", [P, 2, UNIT, GROUP], BF16)
        pos_ring = sb("pos_ring", [P, MASK_SLOTS, HALF, GROUP], BF16)
        consts_sb = sb("consts_sb", [P, P + WPT], F32)
        pack_w = sb("pack_w", [P, WPT], BF16)
        s_row = sb("s_row", [P, 2, GROUP], F32)
        cols = sb("cols", [P, 12, NJ], F32)
        one = sb("one", [P, 24], F32)
        mean_row = sb("mean_row", [P, FD], F32)
        bias_row = sb("bias_row", [P, F], F32)
        w1_sb = sb("w1_sb", [P, 2, F], F32)
        part_sums = sb("part_sums", [P, TPG, ROW], F32)
        row_sums = sb("row_sums", [P, TPG, ROW], F32)
        rows_x = sb("rows_x", [P, TPG, F], F32)
        rows_y = sb("rows_y", [P, TPG, F], F32)
        parts = sb("parts", [P, TPG, ROW], F16)
        stats = sb("stats", [P, TPG, 6], F32)
        mv = sb("mv", [P, TPG, 2], F32)
        wh_top = sb("wh_top", [P, NX], F32)
        x_sums = sb("x_sums", [P, NX], F32)
        wide_flag = sb("wide_flag", [P, 1], I32)
        top_low = sb("top_low", [P, 4], F32)
        wide_one = sb("wide_one", [P, 8], F32)

        ident = consts_sb[:, 0:P]
        s_col, t_col, t_big, e_col, f_col, u_col, v_col, y_col, uy_col, vy_col, e_den, f_den = \
            (cols[:, k, :] for k in range(12))
        t_max, _, wh_max, wh_one, neg_t, neg_ft, inv_wh, scale_e, ones, sum_x = (one[:, k:k + 1] for k in range(10))
        t_max, t_spread = top_low[:, 2:3], wide_one[:, 7:8]
        half_max, row_max, neg_max, half_sum, row_sum = (wide_one[:, a:b] for a, b in ((0, 2), (2, 3), (3, 4), (4, 6), (6, 7)))
        minus_half, inv_den, flag, var_eps, rstd, minus_mean, shift = (one[:, k:k + 2] for k in range(10, 24, 2))
        nd = row_sums[:, :, 0:FD]
        hidden = row_sums[:, :, 0:F]
        scaled = row_sums[:, :, FD:FD + F]
        exp_in = part_sums[:, :, 0:F]

        wh = words[:, NG // 2:, :].rearrange("p g w -> p (g w)").bitcast(F32)[:, 0:NJ * F]\
            .rearrange("p (j f) -> p j f", f=F)
        early = words[:, 2:NG // 2, :].rearrange("p g w -> p (g w)").bitcast(F32)
        sizes, at, early_of = dict(product=3 * UNIT * F, wq=F + 2, w_turn=P, a_sb=2,
                                   s_turn=P, sum_xb=P), 0, {}
        for name, size in sizes.items():
            early_of[name] = early[:, at:at + size]
            at += size
        product = early_of["product"].rearrange("p (k j f) -> p k j f", k=3, f=F)
        x_in = factors[:, 1, :, :].rearrange("p j r -> p (j r)").bitcast(F32)[:, 0:X_SLOTS * XB * F]\
            .rearrange("p (k j f) -> p k j f", k=X_SLOTS, f=F)
        x_t = product[:, 2, 0:2 * XB, :].rearrange("p (k j) f -> p k (j f)", k=2)
        wq, w_turn, a_sb, s_turn, sum_xb = (early_of[n] for n in ("wq", "w_turn", "a_sb", "s_turn", "sum_xb"))
        ring_1 = adj_ring[:, :, :, :].rearrange("p s t c -> p (s t c)").bitcast(BF16)\
            .rearrange("p (s j r) -> p s j r", s=RING_1, j=UNIT)
        turned = pos_ring[:, 0, :, :].rearrange("p j r -> p (j r)").bitcast(F32)[:, 0:2 * TPG * P]

        acc = [ctx.enter_context(nc.psum_tensor(f"acc{k}", [P, 512], F32)) for k in range(2 * TPG)]
        pack_ps = [ctx.enter_context(nc.psum_tensor(f"pack_ps{k}", [P, 512], F32)) for k in range(2)]
        turn_ps = [ctx.enter_context(nc.psum_tensor(f"turn_ps{k}", [P, 512], F32)) for k in range(2)]

        consts_in, w0_in, a0_in, w1_in, bias_in = (sem(n) for n in "consts_in w0_in a0_in w1_in bias_in".split())
        x_in_sem = [sem(f"x_in{k}") for k in range(X_SLOTS)]
        adj_in = [sem("adj_in0"), sem("adj_in1")]
        s_row_in = [sem("s_row_in0"), sem("s_row_in1")]
        rows_in, rows1_in = sem("rows_in"), sem("rows1_in")
        parts_in = [sem(f"parts_in{k}") for k in range(NJ // HALF)]
        s_out, x1_out, parts_out, y_out = (sem(n) for n in "s_out x1_out parts_out y_out".split())
        pack_w_ok, ones_ok, half_ok, tail_ok = (sem(n) for n in "pack_w_ok ones_ok half_ok tail_ok".split())
        w0_turned, w_turn_ok, wa_made, wa_ok = (sem(n) for n in "w0_turned w_turn_ok wa_made wa_ok".split())
        x_turned, x_t_ok, wh_made, wh_ok, top_ok = (sem(n) for n in "x_turned x_t_ok wh_made wh_ok top_ok".split())
        s_turned, s_turn_ok, sum_x_ok, sum_xb_ok = (sem(n) for n in "s_turned s_turn_ok sum_x_ok sum_xb_ok".split())
        mean_made, mean_ok, one_row_ok = (sem(n) for n in "mean_made mean_ok one_row_ok".split())
        t_top_ok, t_max_ok, wh_one_ok, wh_max_ok = (sem(n) for n in "t_top_ok t_max_ok wh_one_ok wh_max_ok".split())
        neg_ok, y_ok_col, uy_ok, exp_cols_ok, t_big_ok = (sem(n) for n in "neg_ok y_col_ok uy_ok exp_cols_ok t_big_ok".split())
        guard_ok, inv_ok, scale_ok, den_ok, den_hi_ok = (sem(n) for n in "guard_ok inv_ok scale_ok den_ok den_hi_ok".split())
        ef_ok, product_ok, high_ok, e_low_ok, f_low_ok = (
            sem(n) for n in "ef_ok product_ok high_ok e_low_ok f_low_ok".split())
        packed, words_ok, unpacked = (sem(n) for n in "packed words_ok unpacked".split())
        score_ok, pos_ok, mask_ok, mask_used, acc_done = (sem(n) for n in "score_ok pos_ok mask_ok mask_used acc_done".split())
        pos_copied, neg_added, nd_ok, flag_ok, full_ok, inv_den_ok, hidden_ok, exp_in_ok, exp_ok, elu_ok = (
            sem(n) for n in "pos_copied neg_added nd_ok flag_ok full_ok inv_den_ok hidden_ok exp_in_ok exp_ok elu_ok".split())
        y_ok, stats_ok, mv_ok, var_ok, rstd_ok, minus_ok, shift_ok, x1_ok, high_part, low_part = (
            sem(n) for n in "y_ok stats_ok mv_ok var_ok rstd_ok minus_ok shift_ok x1_ok high_part low_part".split())
        fill_ok, relu_ok, scaled_ok = sem("fill_ok"), sem("relu_ok"), sem("scaled_ok")
        (low_ok, spread_ok, wide_ok, wh_saved, wh_out, w_t_in, w_wh_in, w_adj_in, w_x_in, w_stored, w_parts_in, w_step,
         w_max, w_exp, w_turned, w_copied, w_sum, w_hidden, w_elu_in, w_elu, w_y, w_stats, w_mv, w_var, w_rstd, w_x1, w_high,
         w_low, w_masks) = (sem(n) for n in (
            "low_ok spread_ok wide_ok wh_saved wh_out w_t_in w_wh_in w_adj_in w_x_in w_stored w_parts_in w_step "
            "w_max w_exp w_turned w_copied w_sum w_hidden w_elu_in w_elu w_y w_stats w_mv w_var w_rstd w_x1 w_high "
            "w_low w_masks").split())
        mask1_ok, mask1_used, acc1_done, copied1, nd1_ok, inv1_ok, mean1_ok, turned1, turned1_ok, proj1_ok, xb1_ok = (
            sem(n) for n in ("mask1_ok mask1_used acc1_done copied1 nd1_ok inv1_ok mean1_ok turned1 turned1_ok "
                             "proj1_ok xb1_ok").split())
        y1_ok, stats1_ok, mv1_ok, var1_ok, rstd1_ok, out_ok = (
            sem(n) for n in "y1_ok stats1_ok mv1_ok var1_ok rstd1_ok out_ok".split())

        x_tiles = x.rearrange("(j p) f -> p j f", p=P)
        adj_tiles = adj.rearrange("(g k t w) c -> g t k w c", g=NG, k=BITS, t=TPG)
        out_rows = out.rearrange("(g b p) f -> g p b f", g=NG, p=P)
        x_rows = x.rearrange("(g b p) f -> g p b f", g=NG, p=P)
        x1_rows = x1_dram.rearrange("(g b p) f -> g p b f", g=NG, p=P)
        parts_rows = parts_dram.rearrange("(g b p) f -> g p b f", g=NG, p=P)
        parts_tiles = parts_dram.rearrange("(j p) f -> p j f", p=P)
        s_rows = s_dram[0:NJ, :].rearrange("(g j) p -> g (j p)", g=NG)
        t_row_dram = s_dram[NJ:2 * NJ, :].rearrange("j p -> (j p)")
        adj_rows = adj.rearrange("(i p) c -> i p c", p=P)
        x_tile, x1_tile, parts_tile = (d.rearrange("(i p) f -> i p f", p=P) for d in (x, x1_dram, parts_dram))
        wide_f32 = factors[:, :, :, :].rearrange("p k j r -> p (k j r)").bitcast(F32)
        t_all = wide_f32[:, 0:N]
        wh_all = wide_f32[:, N:N + NJ * F].rearrange("p (j f) -> p j f", f=F)
        adj_all = adj_ring[:, :, :, :].rearrange("p s t c -> p (s t c)")
        adj_01 = adj_all.bitcast(F32)
        prob = [r[:, :, :, :].rearrange("p a j r -> p (a j r)").bitcast(F32) for r in (neg_ring, pos_ring)]
        prob_t = [s_row[:, :, :].rearrange("p k r -> p (k r)"),
                  part_sums[:, :, :].rearrange("p b r -> p (b r)")[:, 0:4 * P]]
        HC = N // 2

        def is_wide(eng):
            eng.wait_ge(wide_ok, 1)
            return eng.value_load(wide_flag[0:1, 0:1], min_val=0, max_val=1)

        block = ctx.enter_context(nc.Block())

        @block.sync
        def _(sp):
            def load_adj(g, c):
                sp.wait_ge(packed, UPG * g + c + 1)
                for t in range(TPG):
                    sp.dma_start(adj_ring[:, c % ADJ_SLOTS, t, :],
                                 adj_tiles[g, t, :, :, c * COLS:(c + 1) * COLS])\
                        .then_inc(adj_in[c % ADJ_SLOTS], 16)

            def load_s(g, slot):
                sp.dma_start(s_row[:, slot, :], s_rows[g, :].partition_broadcast(P)).then_inc(s_row_in[slot], 16)

            def store_x1(g):
                sp.wait_ge(x1_ok, TPG * (g + 1))
                sp.dma_start(x1_rows[g], rows_y[:, :, :]).then_inc(x1_out, 16)
                sp.wait_ge(low_part, g + 1)
                sp.dma_start(parts_rows[g], parts[:, :, :]).then_inc(parts_out, 16)

            def load_x(g, first=False):
                if not first:
                    sp.wait_ge(y_ok, g)
                sp.dma_start(rows_x[:, :, :], x_rows[g]).then_inc(rows_in, 16)

            sp.sem_inc(packed, ADJ_SLOTS)
            sp.dma_start(consts_sb[:, :], consts).then_inc(consts_in, 16)
            sp.dma_start(wq[:, 0:F], w0).then_inc(w0_in, 16)
            sp.dma_start(a_sb, a0.rearrange("(k f) o -> f (k o)", k=2), allow_slow_non_contiguous=True).then_inc(a0_in, 16)
            for k in range(X_SLOTS):
                sp.dma_start(x_in[:, k], x_tiles[:, XB * k:XB * (k + 1), :]).then_inc(x_in_sem[k], 16)
            load_adj(0, 0)
            with sp.Fori(1, NX // X_SLOTS) as n:
                for k in range(X_SLOTS):
                    sp.wait_ge(x_turned, X_SLOTS * (n - 1) + k + 1)
                    sp.dma_start(x_in[:, k], x_tiles[:, bass.ds(XB * (X_SLOTS * n + k), XB), :])\
                        .then_inc(x_in_sem[k], 16)
            load_adj(0, 1)
            load_adj(0, 2)
            sp.dma_start(w1_sb[:, :, :], w1.rearrange("(k f) o -> f k o", k=2)).then_inc(w1_in, 16)
            sp.dma_start(bias_row[:, :], b1.partition_broadcast(P)).then_inc(bias_in, 16)
            sp.wait_ge(s_turn_ok, 1)
            sp.dma_start(s_dram, s_turn).then_inc(s_out, 16)
            sp.wait_ge(s_out, 16)
            load_s(0, 0)
            load_s(1, 1)
            load_adj(0, 3)
            load_x(0, True)
            wide = is_wide(sp)
            with sp.If(wide > 0):
                sp.dma_start(wh_dram.rearrange("(j p) f -> p j f", p=P), wh).then_inc(wh_out, 16)
                sp.wait_ge(wh_out, 16)
            sp.sem_inc(wh_saved, 1)

            def group(g, slot, first=False, adj_next=True, s_next=True):
                if adj_next:
                    for c in range(UPG):
                        load_adj(g + 1, c)
                if not first:
                    store_x1(g - 1)
                    load_x(g)
                if s_next:
                    sp.wait_ge(score_ok, 8 * (g + 1))
                    load_s(g + 2, slot)

            group(0, 0, first=True)
            with sp.Fori(0, NG // 2 - 2) as n:
                group(2 * n + 1, 1)
                group(2 * n + 2, 0)
            group(NG - 3, 1)
            group(NG - 2, 0, s_next=False)

            GPH = HALF // TPG
            for k in range(NJ // HALF):
                sp.wait_ge(mask_used, 8 * (NG - 1) + k + 1 + MASK_SLOTS)
                if k == NJ // HALF - 2:
                    store_x1(NG - 2)
                    load_x(NG - 1)
                if k == NJ // HALF - 1:
                    store_x1(NG - 1)
                sp.wait_ge(parts_out, 16 * GPH * (k + 1))
                sp.dma_start(factors[:, 0, HALF * k:HALF * (k + 1), :], parts_tiles[:, HALF * k:HALF * (k + 1), :])\
                    .then_inc(parts_in[k], 16)
            sp.wait_ge(x1_out, 16 * NG)

            def wide_loads(i):
                sp.wait_ge(w_max, i + 1)
                sp.dma_start(adj_all, adj_rows[i]).then_inc(w_adj_in, 16)
                sp.wait_ge(w_y, i + 1)
                sp.dma_start(rows_x[:, 0, :], x_tile[i]).then_inc(w_x_in, 16)

            with sp.If(wide > 0):
                for k in range(NJ // HALF):
                    sp.wait_ge(parts_in[k], 16)
                sp.wait_ge(mask1_ok, UPG)
                sp.sem_inc(w_max, 1)
                sp.sem_inc(w_y, 1)
                sp.sem_inc(w_stored, 32)
                sp.dma_start(t_all, t_row_dram.partition_broadcast(P)).then_inc(w_t_in, 16)
                sp.dma_start(wh_all, wh_dram.rearrange("(j p) f -> p j f", p=P)).then_inc(w_wh_in, 16)
                with sp.Fori(0, NJ) as i:
                    wide_loads(i)
                    sp.wait_ge(w_x1, i + 1)
                    sp.dma_start(x1_tile[i], rows_y[:, 0, :]).then_inc(w_stored, 16)
                    sp.wait_ge(w_low, i + 1)
                    sp.dma_start(parts_tile[i], parts[:, 0, :]).then_inc(w_stored, 16)
                sp.wait_ge(w_stored, 32 * (NJ + 1))
                sp.dma_start(factors[:, 0, :, :], parts_tiles).then_inc(w_parts_in, 16)

            def rows_1(g):
                sp.dma_start(rows_x[:, :, :], x1_rows[g]).then_inc(rows1_in, 16)

            def store_1(g):
                sp.wait_ge(out_ok, TPG * (g + 1))
                sp.dma_start(out_rows[g], rows_y[:, :, :]).then_inc(y_out, 16)

            rows_1(0)
            with sp.Fori(1, NG) as g:
                sp.wait_ge(turned1, g)
                sp.wait_ge(xb1_ok, g)
                rows_1(g)
                store_1(g - 1)
            store_1(NG - 1)
            sp.wait_ge(y_out, 16 * NG)

        @block.gpsimd
        def _(pool):
            pool.memset(minus_half, -0.5).then_inc(half_ok, 1)
            pool.wait_ge(t_top_ok, 1)
            pool.wait_ge(low_ok, 2)
            pool.partition_all_reduce(top_low[:, 2:4], top_low[:, 0:2], P, bass.bass_isa.ReduceOp.max).then_inc(t_max_ok, 1)
            pool.wait_ge(wh_one_ok, 1)
            pool.partition_all_reduce(wh_max, wh_one, P, bass.bass_isa.ReduceOp.max).then_inc(wh_max_ok, 1)

            def make_product(n):
                c, k = n // 2, n % 2
                js = slice(c * UNIT, (c + 1) * UNIT)
                if n >= 3:
                    pool.wait_ge((e_low_ok, f_low_ok)[(n - 3) % 2], (n - 3) // 2 + 1)
                pool.tensor_tensor(product[:, n % 3, :, :], wh[:, js, :],
                                   (e_col, f_col)[k][:, js].unsqueeze(2).to_broadcast([P, UNIT, F]), ALU.mult)\
                    .then_inc(product_ok, 1)

            def low_of_f(c):
                js = slice(c * UNIT, (c + 1) * UNIT)
                pool.wait_ge(high_ok, 2 * c + 2)
                pool.tensor_tensor(factors[:, 1, js, FD:FD + F], product[:, (2 * c + 1) % 3, :, :],
                                   factors[:, 1, js, 0:F], ALU.subtract).then_inc(f_low_ok, 1)

            pool.wait_ge(ef_ok, 2)
            make_product(0)
            for c in range(UPG):
                make_product(2 * c + 1)
                if c < UPG - 1:
                    make_product(2 * c + 2)
                low_of_f(c)

            def inverse_deviation(n, mv_sem, var_sem, rstd_sem):
                pool.wait_ge(half_ok, 1)
                pool.wait_ge(mv_sem, n)
                pool.tensor_scalar(var_eps, mv[:, :, 1], EPS, None, ALU.add).then_inc(var_sem, TPG)
                pool.wait_ge(var_sem, n)
                pool.tensor_tensor(rstd, var_eps, minus_half, ALU.pow).then_inc(rstd_sem, TPG)

            def softmax_rows(g):
                pool.wait_ge(half_ok, 1)
                pool.wait_ge(neg_added, TPG * (g + 1))
                pool.tensor_tensor(nd, nd, row_sums[:, :, FD:ROW], ALU.add).then_inc(nd_ok, 1)
                for b in range(TPG):
                    pool.wait_ge(mean_ok, 1)
                    pool.wait_ge(flag_ok, g + 1)
                    pool.tensor_scalar(part_sums[:, b, 0:FD], mean_row[:, :], flag[:, b:b + 1], None, ALU.mult)\
                        .then_inc(fill_ok, 1)
                pool.wait_ge(fill_ok, TPG * (g + 1))
                pool.tensor_tensor(nd, nd, part_sums[:, :, 0:FD], ALU.add).then_inc(full_ok, 1)
                for b in range(TPG):
                    pool.wait_ge(half_ok, 1)
                    pool.wait_ge(inv_den_ok, g + 1)
                    pool.tensor_scalar(hidden[:, b, :], hidden[:, b, :], inv_den[:, b:b + 1], wh_one,
                                       ALU.mult, ALU.mult).then_inc(hidden_ok, 1)
                pool.wait_ge(half_ok, 1)
                pool.wait_ge(hidden_ok, TPG * (g + 1))
                pool.tensor_scalar(exp_in, hidden, 0.0, None, ALU.min).then_inc(exp_in_ok, 1)
                pool.wait_ge(half_ok, 1)
                pool.wait_ge(exp_in_ok, g + 1)
                pool.tensor_scalar(hidden, hidden, 0.0, -1.0, ALU.max, ALU.add).then_inc(relu_ok, 1)

            def elu_and_residual(g, first=False):
                pool.wait_ge(relu_ok, g + 1)
                pool.wait_ge(exp_ok, g + 1)
                pool.tensor_tensor(hidden, hidden, exp_in, ALU.add).then_inc(elu_ok, 1)
                pool.wait_ge(elu_ok, g + 1)
                pool.wait_ge(rows_in, 16 * (g + 1))
                if not first:
                    pool.wait_ge(x1_out, 16 * g)
                pool.tensor_tensor(rows_y[:, :, :], hidden, rows_x[:, :, :], ALU.add).then_inc(y_ok, 1)

            def scale_and_shift(g):
                inverse_deviation(TPG * (g + 1), mv_ok, var_ok, rstd_ok)
                pool.tensor_scalar(minus_mean, mv[:, :, 0], -1.0, None, ALU.mult).then_inc(minus_ok, TPG)
                pool.wait_ge(minus_ok, TPG * (g + 1))
                pool.wait_ge(rstd_ok, TPG * (g + 1))
                pool.tensor_tensor(shift, minus_mean, rstd, ALU.mult).then_inc(shift_ok, TPG)

            def low_parts(g):
                pool.wait_ge(half_ok, 1)
                pool.wait_ge(x1_ok, TPG * (g + 1))
                pool.tensor_scalar(scaled, rows_y[:, :, :], X_SCALE, None, ALU.mult).then_inc(scaled_ok, 1)
                pool.wait_ge(scaled_ok, g + 1)
                pool.wait_ge(high_part, g + 1)
                pool.tensor_tensor(parts[:, :, FD:FD + F], scaled, parts[:, :, 0:F], ALU.subtract).then_inc(low_part, 1)

            def output_0(g, first=False):
                softmax_rows(g)
                elu_and_residual(g, first)
                scale_and_shift(g)
                low_parts(g)

            pool.wait_ge(one_row_ok, 1)
            output_0(0, first=True)
            with pool.Fori(1, NG - 1) as g:
                output_0(g)
            scale_and_shift(NG - 1)
            with pool.If(is_wide(pool) > 0):
                with pool.Fori(TPG, TPG * NJ + 1, TPG) as n:
                    inverse_deviation(n, w_mv, w_var, w_rstd)
            with pool.Fori(TPG, TPG * NG + 1, TPG) as n:
                inverse_deviation(n, mv1_ok, var1_ok, rstd1_ok)

        @block.scalar
        def _(act):
            act.wait_ge(consts_in, 16)
            act.activation(pack_w[:, :], consts_sb[:, P:P + WPT], ACT.Copy).then_inc(pack_w_ok, 1)
            act.wait_ge(w0_turned, 1)
            act.activation(w_turn, turn_ps[0][:, 0:P], ACT.Copy).then_inc(w_turn_ok, 1)
            act.wait_ge(wa_made, 1)
            act.activation(wq[:, F:F + 2], turn_ps[1][:, 0:2], ACT.Copy).then_inc(wa_ok, 1)

            def copy_turned(n, first=False):
                for k in range(2):
                    act.wait_ge(x_turned, 2 * n + k + 1)
                    if not first:
                        act.wait_ge(wh_made, 2 * n + k - 1)
                    act.activation(x_t[:, k, :], turn_ps[k][:, :], ACT.Copy,
                                   accum_out=x_sums[:, bass.ds(2 * n + k, 1)]).then_inc(x_t_ok, 1)

            def copy_words(g, c):
                act.wait_ge(packed, UPG * g + c + 1 + ADJ_SLOTS)
                act.activation(words[:, g, c * WPU:(c + 1) * WPU], pack_ps[c % 2][:, 0:WPU], ACT.Copy)\
                    .then_inc(words_ok, 1)

            copy_turned(0, True)
            with act.Fori(1, NX // 2) as n:
                copy_turned(n)
            act.wait_ge(s_turned, 1)
            act.activation(s_turn, turn_ps[0][:, 0:P], ACT.Copy).then_inc(s_turn_ok, 1)
            copy_words(0, 0)
            copy_words(0, 1)

            act.wait_ge(neg_ok, 2)
            act.activation(e_col, t_col, ACT.Exp, bias=neg_t).then_inc(exp_cols_ok, 1)
            act.activation(f_col, t_col, ACT.Exp, bias=neg_ft, scale=ALPHA).then_inc(exp_cols_ok, 1)
            act.wait_ge(uy_ok, 2)
            act.activation(u_col, uy_col, ACT.Exp).then_inc(exp_cols_ok, 1)
            act.activation(v_col, vy_col, ACT.Exp).then_inc(exp_cols_ok, 1)
            act.wait_ge(t_big_ok, 1)

            def scores(g, slot, h):
                act.wait_ge(mask_used, 8 * g + h + 1)
                for j in range(HALF):
                    a = act.activation(pos_ring[:, h % MASK_SLOTS, j, :], s_row[:, slot, :], ACT.Relu,
                                       bias=t_big[:, h * HALF + j:h * HALF + j + 1], scale=BIG)
                a.then_inc(score_ok, 1)

            def copy_positive(g, first=False):
                if not first:
                    act.wait_ge(elu_ok, g)
                for b in range(TPG):
                    act.wait_ge(acc_done, 3 * g + 2 * b + 1)
                    act.activation(part_sums[:, b, :], acc[2 * b][:, 0:ROW], ACT.Copy,
                                   scale=u_col[:, bass.ds(TPG * g + b, 1)]).then_inc(pos_copied, 1)

            def exponential(g):
                act.wait_ge(exp_in_ok, g + 1)
                act.activation(exp_in, exp_in, ACT.Exp).then_inc(exp_ok, 1)

            def high_parts(g, first=False):
                act.wait_ge(x1_ok, TPG * (g + 1))
                if first:
                    act.wait_ge(tail_ok, 2)
                else:
                    act.wait_ge(parts_out, 16 * g)
                act.activation(parts[:, :, 0:F], rows_y[:, :, :], ACT.Copy, scale=X_SCALE).then_inc(high_part, 1)

            def next_words(g, c, last=False):
                if not (last and c >= 2):
                    copy_words(g + c // 2, (c + 2) % UPG)

            def normalise(g, first=False):
                act.wait_ge(shift_ok, TPG * (g + 1))
                if not first:
                    act.wait_ge(low_part, g)
                for b in range(TPG):
                    act.activation(rows_y[:, b, :], rows_y[:, b, :], ACT.Identity, bias=shift[:, b:b + 1],
                                   scale=rstd[:, b:b + 1]).then_inc(x1_ok, 1)

            def group(g, slot, loads, second=False, last=False):
                act.wait_ge(s_row_in[slot], 16 * loads)
                for h in range(8):
                    scores(g, slot, h)
                    if second and h == UPG + 1:
                        act.wait_ge(wh_saved, 1)
                        act.wait_ge(e_low_ok, UPG)
                        act.wait_ge(f_low_ok, UPG)
                    if h % 2:
                        next_words(g, h // 2, last)
                    if h == 2:
                        copy_positive(g - 1, second)
                    if h == 4:
                        exponential(g - 1)
                    if h == 6:
                        normalise(g - 1, second)
                    if h == 7:
                        high_parts(g - 1, second)

            act.wait_ge(s_row_in[0], 16)
            for c in range(UPG):
                for h in (2 * c, 2 * c + 1):
                    scores(0, 0, h)
                for k in range(2):
                    act.wait_ge(product_ok, 2 * c + k + 1)
                    act.activation(factors[:, k, c * UNIT:(c + 1) * UNIT, 0:F], product[:, (2 * c + k) % 3, :, :],
                                   ACT.Copy)\
                        .then_inc(high_ok, 1)
                next_words(0, c)
            group(1, 1, 1, second=True)
            with act.Fori(1, NG // 2 - 1) as n:
                group(2 * n, 0, n + 1)
                group(2 * n + 1, 1, n + 1)
            group(NG - 2, 0, NG // 2)
            group(NG - 1, 1, NG // 2, last=True)
            copy_positive(NG - 1)
            exponential(NG - 1)
            normalise(NG - 1)
            high_parts(NG - 1)

            with act.If(is_wide(act) > 0):
                with act.Fori(0, NJ) as i:
                    act.wait_ge(w_max, i + 2)
                    for k in range(2):
                        act.activation(prob[k], prob[k], ACT.Exp, bias=neg_max, accum_out=half_sum[:, k:k + 1])\
                            .then_inc(w_exp, 1)
                    for q in range(NX):
                        act.wait_ge(w_turned, NX * i + q + 1)
                        act.wait_ge(w_sum, NX * i + q + 1)
                        act.activation(prob_t[q % 2], turn_ps[q % 2][:, :], ACT.Copy).then_inc(w_copied, 1)
                    act.wait_ge(w_elu_in, i + 1)
                    act.activation(mean_row[:, 0:F], mean_row[:, 0:F], ACT.Exp).then_inc(w_elu, 1)
                    act.wait_ge(w_x1, i + 1)
                    act.activation(parts[:, 0, 0:F], rows_y[:, 0, :], ACT.Copy, scale=X_SCALE).then_inc(w_high, 1)

            def copy_sums(g, first=False):
                if first:
                    act.wait_ge(elu_ok, NG)
                else:
                    act.wait_ge(nd1_ok, g)
                act.wait_ge(acc1_done, g + 1)
                act.activation(part_sums[:, 0, :], acc[0][:, 0:ROW], ACT.Copy).then_inc(copied1, 1)
                act.wait_ge(mask1_used, UPG * (g + 1) + RING_1)
                act.activation(part_sums[:, 1, :], acc[1][:, 0:ROW], ACT.Copy).then_inc(copied1, 1)

            def copy_turned_1(g, first=False):
                act.wait_ge(turned1, g + 1)
                if not first:
                    act.wait_ge(proj1_ok, g)
                act.activation(turned, turn_ps[0][:, :], ACT.Copy).then_inc(turned1_ok, 1)

            copy_sums(0, True)
            copy_turned_1(0, True)
            with act.Fori(1, NG) as g:
                copy_sums(g)
                copy_turned_1(g)

        @block.tensor
        def _(pe):
            pe.sem_inc(mask_used, MASK_SLOTS)
            pe.sem_inc(mask1_used, RING_1)
            pe.wait_ge(consts_in, 16)
            pe.wait_ge(w0_in, 16)
            pe.transpose(turn_ps[0][:, 0:P], wq[:, 0:F], ident).then_inc(w0_turned, 1)
            pe.wait_ge(w_turn_ok, 1)
            pe.wait_ge(a0_in, 16)
            pe.matmul(turn_ps[1][:, 0:2], w_turn, a_sb, start=True, stop=True).then_inc(wa_made, 1)
            pe.wait_ge(wa_ok, 1)
            pe.wait_ge(ones_ok, 1)

            def turn_x(n, k, first=False):
                pe.wait_ge(x_in_sem[k], 16 * (n + 1))
                if not first:
                    pe.wait_ge(x_t_ok, X_SLOTS * n + k - 1)
                for j in range(XB):
                    m = pe.transpose(turn_ps[k % 2][:, j * P:(j + 1) * P], x_in[:, k, j, :], ident)
                m.then_inc(x_turned, 1)

            def make_wh(n, k, first=False):
                pe.wait_ge(x_t_ok, X_SLOTS * n + k + 1)
                if not first:
                    pe.wait_ge(wh_ok, X_SLOTS * n + k - 1)
                for j in range(XB):
                    o = (j % 2) * (F + 2)
                    m = pe.matmul(acc[2 * (k % 2) + j // 2][:, o:o + F + 2], x_t[:, k % 2, j * P:(j + 1) * P], wq,
                                  start=True, stop=True)
                m.then_inc(wh_made, 1)

            def wh_steps(n, first=False, last=False):
                for k in range(X_SLOTS):
                    if k + 1 < X_SLOTS:
                        turn_x(n, k + 1, first and k == 0)
                    elif not last:
                        turn_x(n + 1, 0)
                    make_wh(n, k, first and k < 2)

            def packable(g, c, first=False):
                pe.wait_ge(adj_in[c % ADJ_SLOTS], 32 * (UPG // ADJ_SLOTS * g + c // ADJ_SLOTS + 1))
                if not first:
                    pe.wait_ge(words_ok, UPG * g + c - 1)

            def pack(c):
                for j in range(UNIT):
                    for t in range(TPG):
                        o = (j * TPG + t) * WPT
                        low_bytes = adj_ring[:, c % ADJ_SLOTS, t, j * P:(j + 1) * P].bitcast(F8)\
                            .rearrange("p (c b) -> p c b", b=4)[:, :, 0]
                        m = pe.matmul(pack_ps[c % 2][:, o:o + WPT], low_bytes, pack_w[:, :], start=True, stop=True)
                m.then_inc(packed, 1)

            turn_x(0, 0, True)
            wh_steps(0, first=True)
            with pe.Fori(1, NX // X_SLOTS - 1) as n:
                wh_steps(n)
            pe.wait_ge(pack_w_ok, 1)
            packable(0, 0, first=True)
            pack(0)
            wh_steps(NX // X_SLOTS - 1, last=True)
            pe.wait_ge(wh_ok, NX)
            pe.transpose(turn_ps[0][:, 0:P], cols[:, 0:2, :].rearrange("p k j -> p (k j)"), ident).then_inc(s_turned, 1)
            packable(0, 1, first=True)
            pack(1)
            pe.wait_ge(sum_xb_ok, 1)
            pe.matmul(turn_ps[1][:, 0:F], sum_xb, wq[:, 0:F], start=True, stop=True).then_inc(mean_made, 1)
            for c in range(2, UPG):
                packable(0, c)
                pack(c)

            def multiply(g, h, factors_in=False, first=False):
                pe.wait_ge(mask_ok, 8 * g + h + 1)
                for a in range(2 * TPG):
                    b, neg = a // 2, a % 2
                    if factors_in and a < 2:
                        pe.wait_ge((e_low_ok, f_low_ok)[neg], h // 2 + 1)
                    if h == 0 and not first:
                        pe.wait_ge(neg_added if neg else pos_copied, TPG * (g - 1) + b + 1)
                    for j in range(HALF):
                        jj = h * HALF + j
                        mask = neg_ring[:, (h // 2) % 2, (h % 2) * HALF + j, b * P:(b + 1) * P] if neg else \
                            pos_ring[:, h % MASK_SLOTS, j, b * P:(b + 1) * P]
                        m = pe.matmul(acc[a][:, 0:ROW], mask, factors[:, neg, jj, :],
                                      start=(jj == 0), stop=(jj == NJ - 1))
                    if h == 7 and a < 2 * TPG - 1:
                        m.then_inc(acc_done, 1)
                m.then_inc(mask_used, 1)

            def group(g, first=False, last=False):
                for c in range(UPG):
                    for h in (2 * c, 2 * c + 1):
                        if h % 2 and not last:
                            packable(g + 1, c)
                        multiply(g, h, first and h % 2 == 0, first)
                    if not last:
                        pack(c)

            pe.wait_ge(den_hi_ok, 4)
            group(0, first=True)
            with pe.Fori(1, NG - 1) as g:
                group(g)
            group(NG - 1, last=True)

            with pe.If(is_wide(pe) > 0):
                pe.sem_inc(w_sum, 2)
                pe.wait_ge(low_part, NG)
                pe.wait_ge(w_wh_in, 16)

                def wide_turn(i, q):
                    pe.wait_ge(w_copied, NX * i + q + 1)
                    for j in range(XB):
                        tile = prob[q // (NX // 2)][:, (XB * (q % (NX // 2)) + j) * P:(XB * (q % (NX // 2)) + j + 1) * P]
                        m = pe.transpose(turn_ps[q % 2][:, j * P:(j + 1) * P], tile, ident)
                    m.then_inc(w_turned, 1)

                pe.sem_inc(w_copied, 2)
                with pe.Fori(0, NJ) as i:
                    pe.wait_ge(w_exp, 2 * i + 2)
                    pe.wait_ge(w_hidden, i + 1)
                    for q in range(NX):
                        wide_turn(i, q)
                        pe.wait_ge(w_copied, NX * i + q + 3)
                        for j in range(XB):
                            m = pe.matmul(acc[0][:, 0:F], prob_t[q % 2][:, j * P:(j + 1) * P], wh_all[:, XB * q + j, :],
                                          start=(q == 0 and j == 0), stop=(q == NX - 1 and j == XB - 1))
                        m.then_inc(w_sum, 1)
                pe.wait_ge(w_parts_in, 16)
                pe.wait_ge(w_masks, UPG)

            def multiply_1(g, c, first=False):
                pe.wait_ge(mask1_ok, UPG * g + c + 1)
                for b in range(TPG):
                    if c == 0 and first:
                        pe.wait_ge(neg_added if b else pos_copied, TPG * (NG - 1) + 1)
                    elif c == 0:
                        pe.wait_ge(copied1, TPG * (g - 1) + b + 1)
                    for j in range(UNIT):
                        jj = c * UNIT + j
                        if first and b == 0 and j % HALF == 0:
                            pe.wait_ge(parts_in[jj // HALF], 16)
                        m = pe.matmul(acc[b][:, 0:ROW], ring_1[:, c, j, b * P:(b + 1) * P], factors[:, 0, jj, :],
                                      start=(jj == 0), stop=(jj == NJ - 1))
                    if c == UPG - 1 and b == 0:
                        m.then_inc(acc1_done, 1)
                m.then_inc(mask1_used, 1)

            def turn_rows(g, first=False):
                pe.wait_ge(mean1_ok, TPG * (g + 1))
                pe.wait_ge(rows1_in, 16 * (g + 1))
                if not first:
                    pe.wait_ge(turned1_ok, g)
                for k, rows in enumerate((hidden, rows_x)):
                    for b in range(TPG):
                        m = pe.transpose(turn_ps[0][:, (TPG * k + b) * P:(TPG * k + b + 1) * P], rows[:, b, :], ident)
                m.then_inc(turned1, 1)

            def project(g, first=False):
                pe.wait_ge(turned1_ok, g + 1)
                if not first:
                    pe.wait_ge(y1_ok, g)
                for b in range(TPG):
                    for k in range(2):
                        m = pe.matmul(turn_ps[1][:, b * F:(b + 1) * F],
                                      turned[:, (TPG * k + b) * P:(TPG * k + b + 1) * P], w1_sb[:, k, :],
                                      start=(k == 0), stop=(k == 1))
                m.then_inc(proj1_ok, 1)

            def group_1(g, first=False, second=False):
                for c in range(UPG):
                    multiply_1(g, c, first)
                    if c == 0 and not first:
                        turn_rows(g - 1, second)
                    if c == 1 and not first:
                        project(g - 1, second)

            pe.wait_ge(w1_in, 16)
            group_1(0, first=True)
            group_1(1, second=True)
            with pe.Fori(2, NG) as g:
                group_1(g)
            turn_rows(NG - 1)
            project(NG - 1)

        @block.vector
        def _(dve):
            dve.memset(ones, 1.0).then_inc(ones_ok, 1)
            dve.memset(mean_row[:, F:FD], 1.0).then_inc(one_row_ok, 1)
            dve.memset(parts[:, :, F:FD], 1.0).then_inc(tail_ok, 1)
            dve.memset(parts[:, :, ROW - 1:ROW], 0.0).then_inc(tail_ok, 1)

            def copy_wh(n, k):
                dve.wait_ge(wh_made, 2 * n + k + 1)
                for half in range(2):
                    bank = acc[2 * k + half][:, 0:2 * (F + 2)].rearrange("p (j f) -> p j f", j=2)
                    j0 = 2 * XB * n + XB * k + 2 * half
                    dve.tensor_copy(wh[:, bass.ds(j0, 2), :], bank[:, :, 0:F])
                    d = dve.tensor_copy(cols[:, 0:2, bass.ds(j0, 2)], bank[:, :, F:F + 2].rearrange("p j k -> p k j"))
                d.then_inc(wh_ok, 1)
                dve.wait_ge(wh_ok, 2 * n + k + 1)
                dve.tensor_reduce(wh_top[:, bass.ds(2 * n + k, 1)], wh[:, bass.ds(2 * XB * n + XB * k, XB), :], AX.XY,
                                  ALU.max, apply_absolute_value=True).then_inc(top_ok, 1)

            with dve.Fori(0, NX // 2) as n:
                for k in range(2):
                    copy_wh(n, k)
            dve.tensor_reduce(top_low[:, 0:1], t_col, AX.X, ALU.max).then_inc(t_top_ok, 1)
            dve.tensor_reduce(top_low[:, 1:2], t_col, AX.X, ALU.min).then_inc(low_ok, 1)
            dve.wait_ge(low_ok, 1)
            dve.tensor_scalar(top_low[:, 1:2], top_low[:, 1:2], -1.0, None, ALU.mult).then_inc(low_ok, 1)
            dve.wait_ge(top_ok, NX)
            dve.tensor_reduce(wh_one, wh_top[:, :], AX.X, ALU.max).then_inc(wh_one_ok, 1)
            dve.tensor_scalar(t_big, t_col, BIG, None, ALU.mult).then_inc(t_big_ok, 1)
            dve.wait_ge(x_t_ok, NX)
            dve.tensor_reduce(sum_x, x_sums[:, :], AX.X, ALU.add).then_inc(sum_x_ok, 1)
            dve.wait_ge(sum_x_ok, 1)
            dve.tensor_scalar(sum_xb, ident, 0.0, sum_x, ALU.mult, ALU.add).then_inc(sum_xb_ok, 1)

            dve.wait_ge(t_max_ok, 1)
            dve.tensor_scalar(neg_t, t_max, -1.0, None, ALU.mult).then_inc(neg_ok, 1)
            dve.tensor_scalar(neg_ft, t_max, -ALPHA, None, ALU.mult).then_inc(neg_ok, 1)
            dve.tensor_scalar(y_col, s_col, t_max, None, ALU.add).then_inc(y_ok_col, 1)
            dve.tensor_scalar(t_spread, t_max, top_low[:, 3:4], None, ALU.add).then_inc(spread_ok, 1)
            dve.wait_ge(spread_ok, 1)
            dve.tensor_scalar(wide_flag[:, :], t_spread, WIDEST, None, ALU.is_gt).then_inc(wide_ok, 1)
            dve.wait_ge(y_ok_col, 1)
            dve.tensor_scalar(uy_col, y_col, 1.0 - ALPHA, 0.0, ALU.mult, ALU.min).then_inc(uy_ok, 1)
            dve.tensor_scalar(vy_col, y_col, ALPHA - 1.0, 0.0, ALU.mult, ALU.min).then_inc(uy_ok, 1)
            dve.wait_ge(wh_max_ok, 1)
            dve.tensor_scalar(wh_one, wh_max, 1e-30, None, ALU.max).then_inc(guard_ok, 1)
            dve.wait_ge(guard_ok, 1)
            dve.reciprocal(inv_wh, wh_one).then_inc(inv_ok, 1)
            dve.wait_ge(inv_ok, 1)
            dve.tensor_scalar(scale_e, inv_wh, E_SCALE, None, ALU.mult).then_inc(scale_ok, 1)
            dve.wait_ge(exp_cols_ok, 2)
            dve.wait_ge(scale_ok, 1)
            for k, (col, den) in enumerate(((e_col, e_den), (f_col, f_den))):
                dve.tensor_scalar(den, col, E_SCALE, None, ALU.mult).then_inc(den_ok, 1)
                dve.wait_ge(den_ok, k + 1)
                dve.tensor_copy(factors[:, k, :, F], den).then_inc(den_hi_ok, 1)
                dve.wait_ge(den_hi_ok, 2 * k + 1)
                dve.tensor_tensor(factors[:, k, :, ROW - 1], den, factors[:, k, :, F], ALU.subtract)\
                    .then_inc(den_hi_ok, 1)
                dve.tensor_scalar(col, col, scale_e, None, ALU.mult).then_inc(ef_ok, 1)

            def unpack(g, c, ring, slot, bits=range(BITS)):
                src = words[:, g, c * WPU:(c + 1) * WPU].rearrange("p (j w) -> p j w", j=UNIT)
                dst = ring[:, slot, :, :].bitcast(U16)
                for k in bits:
                    to = dst[:, :, k * WPG:(k + 1) * WPG]
                    if k < 14:
                        d = dve.tensor_scalar(to, src, 14 - k, 0x4000, ALU.logical_shift_left, ALU.bitwise_and)
                    else:
                        d = dve.tensor_scalar(to, src, k - 14, 0x4000, ALU.logical_shift_right, ALU.bitwise_and)
                return d

            def masks(g, c, output=None, second=False):
                dve.wait_ge(mask_used, 8 * g + 2 * c + 2)
                dve.wait_ge(words_ok, UPG * g + c + 1)
                if output == "sums":
                    add_negative(g - 1, second)
                unpack(g, c, neg_ring, c % 2, range(0, 4))
                unpack(g, c, neg_ring, c % 2, range(4, 8))
                unpack(g, c, neg_ring, c % 2, range(8, 12))
                if output == "sums":
                    find_empty(g - 1)
                unpack(g, c, neg_ring, c % 2, range(12, 16)).then_inc(unpacked, 1)
                positive(g, c, 0)
                if output == "sums":
                    invert_sum(g - 1)
                elif output == "statistics":
                    statistics(g - 1, stats_ok)
                positive(g, c, 1)
                if output == "statistics":
                    aggregate(g - 1, stats_ok, mv_ok)
                for k in range(2):
                    dve.wait_ge(pos_ok, 8 * g + 2 * c + k + 1)
                    neg = neg_ring[:, c % 2, k * HALF:(k + 1) * HALF, :]
                    dve.tensor_tensor(neg, neg, pos_ring[:, (2 * c + k) % MASK_SLOTS, :, :], ALU.subtract)\
                        .then_inc(mask_ok, 1)

            def positive(g, c, k):
                dve.wait_ge(unpacked, UPG * g + c + 1)
                dve.wait_ge(score_ok, 8 * g + 2 * c + k + 1)
                pos = pos_ring[:, (2 * c + k) % MASK_SLOTS, :, :]
                dve.tensor_tensor(pos, pos, neg_ring[:, c % 2, k * HALF:(k + 1) * HALF, :], ALU.min).then_inc(pos_ok, 1)

            def low_of_e(c):
                js = slice(c * UNIT, (c + 1) * UNIT)
                dve.wait_ge(high_ok, 2 * c + 1)
                dve.tensor_tensor(factors[:, 0, js, FD:FD + F], product[:, 2 * c % 3, :, :], factors[:, 0, js, 0:F],
                                  ALU.subtract).then_inc(e_low_ok, 1)

            def add_negative(g, first=False):
                if not first:
                    dve.wait_ge(low_part, g)
                for b in range(TPG):
                    dve.wait_ge(pos_copied, TPG * g + b + 1)
                    if b == 0:
                        dve.wait_ge(acc_done, 3 * g + 2)
                    else:
                        dve.wait_ge(mask_used, 8 * (g + 1) + MASK_SLOTS)
                    dve.scalar_tensor_tensor(out=row_sums[:, b, :], in0=acc[2 * b + 1][:, 0:ROW],
                                             scalar=v_col[:, bass.ds(TPG * g + b, 1)], in1=part_sums[:, b, :],
                                             op0=ALU.mult, op1=ALU.add).then_inc(neg_added, 1)

            def find_empty(g):
                dve.wait_ge(nd_ok, g + 1)
                dve.tensor_scalar(flag, row_sums[:, :, F], 0.0, None, ALU.is_equal).then_inc(flag_ok, 1)

            def invert_sum(g):
                dve.wait_ge(full_ok, g + 1)
                dve.reciprocal(inv_den, row_sums[:, :, F]).then_inc(inv_den_ok, 1)

            def statistics(g, stats_sem, rows_ok=None):
                dve.wait_ge(y_ok if rows_ok is None else rows_ok, g + 1)
                for b in range(TPG):
                    d = dve.bn_stats(stats[:, b, :], rows_y[:, b, :])
                d.then_inc(stats_sem, 1)

            def aggregate(g, stats_sem, mv_sem):
                dve.wait_ge(ones_ok, 1)
                dve.wait_ge(stats_sem, g + 1)
                for b in range(TPG):
                    dve.bn_aggr(mv[:, b, :], stats[:, b, :]).then_inc(mv_sem, 1)

            def normalise(g, rstd_sem, done):
                dve.wait_ge(rstd_sem, TPG * (g + 1))
                for b in range(TPG):
                    dve.tensor_scalar(rows_y[:, b, :], rows_y[:, b, :], mv[:, b, 0:1], rstd[:, b:b + 1],
                                      ALU.subtract, ALU.mult).then_inc(done, 1)

            def group(g, second=False):
                masks(g, 0)
                masks(g, 1, "sums", second)
                masks(g, 2, "statistics")
                masks(g, 3)

            for c in range(UPG):
                masks(0, c)
                low_of_e(c)
            dve.wait_ge(mean_made, 1)
            dve.tensor_scalar(mean_row[:, 0:F], turn_ps[1][:, 0:F], 1.0 / N, inv_wh, ALU.mult, ALU.mult)\
                .then_inc(mean_ok, 1)
            dve.wait_ge(exp_cols_ok, 4)
            dve.wait_ge(mean_ok, 1)
            dve.wait_ge(one_row_ok, 1)
            group(1, second=True)
            with dve.Fori(2, NG - 1) as g:
                group(g)
            group(NG - 1)

            def masks_1(g, c):
                dve.wait_ge(mask1_used, UPG * g + c + 1)
                unpack(g, c, ring_1, c).then_inc(mask1_ok, 1)

            def means_1(g, first=False):
                dve.wait_ge(copied1, TPG * (g + 1))
                if not first:
                    dve.wait_ge(turned1, g)
                dve.tensor_tensor(nd, part_sums[:, :, 0:FD], part_sums[:, :, FD:ROW], ALU.add).then_inc(nd1_ok, 1)
                dve.wait_ge(nd1_ok, g + 1)
                dve.reciprocal(inv_den, row_sums[:, :, F]).then_inc(inv1_ok, 1)
                dve.wait_ge(inv1_ok, g + 1)
                for b in range(TPG):
                    dve.tensor_scalar(hidden[:, b, :], hidden[:, b, :], inv_den[:, b:b + 1], 1.0 / X_SCALE,
                                      ALU.mult, ALU.mult).then_inc(mean1_ok, 1)

            def add_bias(g, first=False):
                dve.wait_ge(rows1_in, 16 * (g + 1))
                if not first:
                    dve.wait_ge(y_out, 16 * g)
                dve.tensor_tensor(rows_y[:, :, :], rows_x[:, :, :], bias_row[:, :].unsqueeze(1).to_broadcast([P, TPG, F]),
                                  ALU.add).then_inc(xb1_ok, 1)

            def output_1(g):
                dve.wait_ge(xb1_ok, g + 1)
                dve.wait_ge(proj1_ok, g + 1)
                dve.tensor_tensor(rows_y[:, :, :], turn_ps[1][:, 0:TPG * F].rearrange("p (b f) -> p b f", b=TPG),
                                  rows_y[:, :, :], ALU.add).then_inc(y1_ok, 1)
                statistics(g, stats1_ok, y1_ok)
                aggregate(g, stats1_ok, mv1_ok)
                normalise(g, rstd1_ok, out_ok)

            def finish_layer_0():
                add_negative(NG - 1)
                dve.wait_ge(neg_added, TPG * NG)
                dve.tensor_tensor(nd, nd, row_sums[:, :, FD:ROW], ALU.add).then_inc(nd_ok, 1)
                find_empty(NG - 1)
                dve.wait_ge(flag_ok, NG)
                for b in range(TPG):
                    d = dve.scalar_tensor_tensor(out=nd[:, b, :], in0=mean_row[:, :], scalar=flag[:, b:b + 1],
                                                 in1=nd[:, b, :], op0=ALU.mult, op1=ALU.add)
                d.then_inc(full_ok, 1)
                invert_sum(NG - 1)
                dve.wait_ge(inv_den_ok, NG)
                for b in range(TPG):
                    dve.tensor_scalar(hidden[:, b, :], hidden[:, b, :], inv_den[:, b:b + 1], wh_one,
                                      ALU.mult, ALU.mult).then_inc(hidden_ok, 1)
                dve.wait_ge(hidden_ok, TPG * NG)
                dve.tensor_scalar(exp_in, hidden, 0.0, None, ALU.min).then_inc(exp_in_ok, 1)
                dve.wait_ge(exp_ok, NG)
                dve.scalar_tensor_tensor(out=hidden, in0=hidden, scalar=0.0, in1=exp_in, op0=ALU.max, op1=ALU.add)\
                    .then_inc(elu_ok, 1)
                dve.wait_ge(elu_ok, NG)
                dve.wait_ge(rows_in, 16 * NG)
                dve.wait_ge(x1_out, 16 * (NG - 1))
                dve.scalar_tensor_tensor(out=rows_y[:, :, :], in0=hidden, scalar=-1.0, in1=rows_x[:, :, :],
                                         op0=ALU.add, op1=ALU.add).then_inc(y_ok, 1)
                statistics(NG - 1, stats_ok)
                aggregate(NG - 1, stats_ok, mv_ok)
                dve.wait_ge(high_part, NG)
                dve.scalar_tensor_tensor(out=parts[:, :, FD:FD + F], in0=rows_y[:, :, :], scalar=X_SCALE,
                                         in1=parts[:, :, 0:F], op0=ALU.mult, op1=ALU.subtract).then_inc(low_part, 1)

            for c in range(UPG):
                masks_1(0, c)
            finish_layer_0()

            def wide_tile(i):
                steps = [0]
                STEPS = 18

                def then(instruction):
                    steps[0] += 1
                    instruction.then_inc(w_step, 1)
                    dve.wait_ge(w_step, STEPS * i + steps[0])

                dve.wait_ge(w_adj_in, 16 * (i + 1))
                dve.wait_ge(w_sum, NX * i + 2)
                for k in range(2):
                    p, c = prob[k], slice(k * HC, (k + 1) * HC)
                    then(dve.tensor_scalar(p, t_all[:, c], cols[:, 0, bass.ds(i, 1)], None, ALU.add))
                    then(dve.scalar_tensor_tensor(out=p, in0=p, scalar=ALPHA, in1=p, op0=ALU.mult, op1=ALU.max))
                    then(dve.tensor_scalar(adj_01[:, c], adj_all[:, c], 0, None, ALU.is_gt))
                    then(dve.tensor_tensor(p, p, adj_01[:, c], ALU.mult))
                    then(dve.tensor_scalar(adj_01[:, c], adj_01[:, c], -1.0, MASKED, ALU.add, ALU.mult))
                    then(dve.tensor_tensor(p, p, adj_01[:, c], ALU.add))
                    then(dve.tensor_reduce(half_max[:, k:k + 1], p, AX.X, ALU.max))
                then(dve.tensor_reduce(row_max, half_max, AX.X, ALU.max))
                dve.tensor_scalar(neg_max, row_max, -1.0, None, ALU.mult).then_inc(w_max, 1)
                dve.wait_ge(w_exp, 2 * i + 2)
                then(dve.tensor_reduce(row_sum, half_sum, AX.X, ALU.add))
                then(dve.reciprocal(row_sum, row_sum))
                dve.wait_ge(w_sum, NX * (i + 1) + 2)
                dve.tensor_scalar(hidden[:, 0, :], acc[0][:, 0:F], row_sum, None, ALU.mult).then_inc(w_hidden, 1)
                dve.wait_ge(w_hidden, i + 2)
                dve.tensor_scalar(mean_row[:, 0:F], hidden[:, 0, :], 0.0, None, ALU.min).then_inc(w_elu_in, 1)
                dve.wait_ge(w_elu, i + 1)
                then(dve.scalar_tensor_tensor(out=hidden[:, 0, :], in0=hidden[:, 0, :], scalar=0.0,
                                              in1=mean_row[:, 0:F], op0=ALU.max, op1=ALU.add))
                dve.wait_ge(w_x_in, 16 * (i + 1))
                dve.wait_ge(w_stored, 32 * i + 32)
                dve.scalar_tensor_tensor(out=rows_y[:, 0, :], in0=hidden[:, 0, :], scalar=-1.0, in1=rows_x[:, 0, :],
                                         op0=ALU.add, op1=ALU.add).then_inc(w_y, 1)
                dve.wait_ge(w_y, i + 2)
                dve.bn_stats(stats[:, 0, :], rows_y[:, 0, :]).then_inc(w_stats, 1)
                dve.wait_ge(ones_ok, 1)
                dve.wait_ge(w_stats, i + 1)
                dve.bn_aggr(mv[:, 0, :], stats[:, 0, :]).then_inc(w_mv, TPG)
                dve.wait_ge(w_rstd, TPG * (i + 1))
                dve.tensor_scalar(rows_y[:, 0, :], rows_y[:, 0, :], mv[:, 0, 0:1], rstd[:, 0:1],
                                  ALU.subtract, ALU.mult).then_inc(w_x1, 1)
                dve.wait_ge(w_x1, i + 1)
                dve.wait_ge(w_high, i + 1)
                dve.scalar_tensor_tensor(out=parts[:, 0, FD:FD + F], in0=rows_y[:, 0, :], scalar=X_SCALE,
                                         in1=parts[:, 0, 0:F], op0=ALU.mult, op1=ALU.subtract).then_inc(w_low, 1)
                assert steps[0] == STEPS

            with dve.If(is_wide(dve) > 0):
                dve.wait_ge(w_t_in, 16)
                dve.sem_inc(w_hidden, 1)
                with dve.Fori(0, NJ) as i:
                    wide_tile(i)
                for c in range(UPG):
                    unpack(0, c, ring_1, c).then_inc(w_masks, 1)

            dve.wait_ge(bias_in, 16)
            dve.wait_ge(x1_out, 16 * NG)

            def group_1(g, first=False):
                for c in range(UPG):
                    if c == UPG // 2:
                        means_1(g - 1, first)
                        add_bias(g - 1, first)
                    masks_1(g, c)
                output_1(g - 1)

            group_1(1, first=True)
            with dve.Fori(2, NG) as g:
                group_1(g)
            means_1(NG - 1)
            add_bias(NG - 1)
            output_1(NG - 1)


def kernel(x, adj, L0_gnn_W, L0_gnn_a, L1_gnn_weight, L1_gnn_bias):
    import numpy as _np
    import concourse.bacc as _bacc
    from concourse import mybir as _mybir
    from concourse.bass_utils import run_bass_kernel_spmd as _run

    consts = _np.zeros((P, P + WPT), _np.float32)
    consts[:, :P] = _np.eye(P)
    for p in range(P):
        consts[p, P + p % WPT] = 2.0 ** (p // WPT) / F8_ONE

    nc = _bacc.Bacc("TRN2", target_bir_lowering=False, num_devices=1)
    arrays, args = {}, []
    for name, a in (("x", x), ("adj", adj), ("w0", L0_gnn_W), ("a0", L0_gnn_a), ("w1", L1_gnn_weight),
                    ("b1", L1_gnn_bias), ("consts", consts)):
        a = _np.ascontiguousarray(a)
        arrays[f"in_{name}"] = a
        args.append(nc.dram_tensor(f"in_{name}", a.shape, _mybir.dt.from_np(a.dtype), kind="ExternalInput").ap())
    args.append(nc.dram_tensor("out_0", x.shape, _mybir.dt.float32, kind="ExternalOutput").ap())
    adj_resnorm_kernel(nc, *args)
    r = _run(nc, [arrays], core_ids=[0])
    return r.results[0]["out_0"]
```
